# Optimizing a Trainium2 kernel written in Bass

```python
import numpy as np
import jax
import jax.numpy as jnp

def _softmax(x, axis=-1):
    return jax.nn.softmax(x, axis=axis)

def _gelu(x):
    return jax.nn.gelu(x, approximate=True)

def _silu(x):
    return jax.nn.silu(x)

def _sigmoid(x):
    return jax.nn.sigmoid(x)

def _layernorm(x, axis=-1, eps=1e-05):
    m = jnp.mean(x, axis=axis, keepdims=True)
    v = jnp.var(x, axis=axis, keepdims=True)
    return (x - m) / jnp.sqrt(v + eps)

def _scatter_add(tgt, idx, src, axis=0):
    return tgt.at[idx].add(src)

def _segment_sum(src, seg, n):
    return jax.ops.segment_sum(src, seg, n)
kernel_name = 'mk_lm_tower_d1_tok_ids256_r4_4b3253'

def setup_inputs(seed: int=0):
    np.random.seed(seed)
    _w = jnp.asarray

    def _rec_inputs():
        import jax
        import jax.numpy as jnp
        _rk = jax.random.key(seed)
        x = jax.random.randint(jax.random.fold_in(_rk, 1), (64, 256), 0, 12564, jnp.int32)
        return x
    x = _rec_inputs()

    def _L0_tok_setup():
        import jax, jax.numpy as jnp
        import numpy as np
        INP_SIZE = 50257
        HIDDEN = 64
        KSIZE = 9
        B, T = (16, 1024)
        key = jax.random.key(seed)
        k1, k2, k3, k4 = jax.random.split(key, 4)
        x = jax.random.randint(k1, (B, T), 0, INP_SIZE, dtype=jnp.int64 if jax.config.jax_enable_x64 else jnp.int32)
        emb = jax.random.normal(k2, (INP_SIZE, HIDDEN), dtype=jnp.float32) * 0.02
        fan_in = HIDDEN * KSIZE
        bound = 1.0 / np.sqrt(fan_in)
        W = jax.random.uniform(k3, (HIDDEN, HIDDEN, KSIZE), dtype=jnp.float32, minval=-bound, maxval=bound)
        b = jax.random.uniform(k4, (HIDDEN,), dtype=jnp.float32, minval=-bound, maxval=bound)
        return {'x': x, 'emb': emb, 'W': W, 'b': b}
    _L0_tok_all = _L0_tok_setup()
    _L0_tok_in = {k: v for k, v in _L0_tok_all.items() if k in ('emb', 'W', 'b')}
    del _L0_tok_all

    def _L0_attn_setup():
        import jax, jax.numpy as jnp
        import numpy as np
        import math
        PI = math.pi

        def _encode_phase(x, w1, b1, w2, b2):
            h = jnp.tanh(jnp.einsum('bld,ed->ble', x, w1) + b1)
            return jnp.tanh(jnp.einsum('bld,kd->blk', h, w2) + b2) * PI
        key = jax.random.key(seed)
        ks = jax.random.split(key, 12)
        B, L, D, K = (2, 512, 64, 32)
        s = 0.02
        return {'x': jax.random.normal(ks[0], (B, L, D), dtype=jnp.float32), 'kw1': jax.random.normal(ks[1], (D, D), dtype=jnp.float32) * s, 'kb1': jnp.zeros((D,), dtype=jnp.float32), 'kw2': jax.random.normal(ks[2], (K, D), dtype=jnp.float32) * s, 'kb2': jnp.zeros((K,), dtype=jnp.float32), 'qw1': jax.random.normal(ks[3], (D, D), dtype=jnp.float32) * s, 'qb1': jnp.zeros((D,), dtype=jnp.float32), 'qw2': jax.random.normal(ks[4], (K, D), dtype=jnp.float32) * s, 'qb2': jnp.zeros((K,), dtype=jnp.float32), 'vw': jax.random.normal(ks[5], (D, D), dtype=jnp.float32) * s, 'vb': jnp.zeros((D,), dtype=jnp.float32)}
    _L0_attn_all = _L0_attn_setup()
    _L0_attn_in = {k: v for k, v in _L0_attn_all.items() if k in ('kw1', 'kb1', 'kw2', 'kb2', 'qw1', 'qb1', 'qw2', 'qb2', 'vw', 'vb')}
    del _L0_attn_all

    def _L0_ffn_setup():
        import jax, jax.numpy as jnp
        import numpy as np
        C = 64
        HID = 256
        E = 8
        TEMP = 1.0
        key = jax.random.key(seed)
        ks = jax.random.split(key, 7)
        x = jax.random.normal(ks[0], (8, 4096, C), dtype=jnp.float32)
        W1 = jax.random.normal(ks[1], (C, HID), dtype=jnp.float32) * 0.02
        b1 = jnp.zeros((HID,), dtype=jnp.float32)
        Wg = jax.random.normal(ks[2], (HID, E), dtype=jnp.float32) * 0.02
        bg = jnp.zeros((E,), dtype=jnp.float32)
        Wd = jax.random.normal(ks[3], (E, HID, C), dtype=jnp.float32) * 0.02
        bd = jnp.zeros((E, C), dtype=jnp.float32)
        return {'x': x, 'W1': W1, 'b1': b1, 'Wg': Wg, 'bg': bg, 'Wd': Wd, 'bd': bd}
    _L0_ffn_all = _L0_ffn_setup()
    _L0_ffn_in = {k: v for k, v in _L0_ffn_all.items() if k in ('W1', 'b1', 'Wg', 'bg', 'Wd', 'bd')}
    del _L0_ffn_all
    return {'x': x, 'L0_tok_emb': _L0_tok_in['emb'], 'L0_tok_W': _L0_tok_in['W'], 'L0_tok_b': _L0_tok_in['b'], 'L0_attn_kw1': _L0_attn_in['kw1'], 'L0_attn_kb1': _L0_attn_in['kb1'], 'L0_attn_kw2': _L0_attn_in['kw2'], 'L0_attn_kb2': _L0_attn_in['kb2'], 'L0_attn_qw1': _L0_attn_in['qw1'], 'L0_attn_qb1': _L0_attn_in['qb1'], 'L0_attn_qw2': _L0_attn_in['qw2'], 'L0_attn_qb2': _L0_attn_in['qb2'], 'L0_attn_vw': _L0_attn_in['vw'], 'L0_attn_vb': _L0_attn_in['vb'], 'L0_ffn_W1': _L0_ffn_in['W1'], 'L0_ffn_b1': _L0_ffn_in['b1'], 'L0_ffn_Wg': _L0_ffn_in['Wg'], 'L0_ffn_bg': _L0_ffn_in['bg'], 'L0_ffn_Wd': _L0_ffn_in['Wd'], 'L0_ffn_bd': _L0_ffn_in['bd']}

def reference(x, L0_tok_emb, L0_tok_W, L0_tok_b, L0_attn_kw1, L0_attn_kb1, L0_attn_kw2, L0_attn_kb2, L0_attn_qw1, L0_attn_qb1, L0_attn_qw2, L0_attn_qb2, L0_attn_vw, L0_attn_vb, L0_ffn_W1, L0_ffn_b1, L0_ffn_Wg, L0_ffn_bg, L0_ffn_Wd, L0_ffn_bd):
    import jax
    import jax.numpy as jnp

    def _L0_tok_ref(x, emb, W, b):
        import jax, jax.numpy as jnp
        import numpy as np
        INP_SIZE = 50257
        HIDDEN = 64
        KSIZE = 9
        B, T = (16, 1024)
        offsets = jnp.arange(-(KSIZE // 2), KSIZE // 2 + 1)
        idx = jnp.clip(x[..., None] + offsets, 0, INP_SIZE - 1)
        gathered = emb[idx]
        out = jnp.einsum('btkh,ohk->bto', gathered, W) + b
        return out

    def _L0_attn_ref(x, kw1, kb1, kw2, kb2, qw1, qb1, qw2, qb2, vw, vb):
        import jax, jax.numpy as jnp
        import numpy as np
        import math
        PI = math.pi

        def _encode_phase(x, w1, b1, w2, b2):
            h = jnp.tanh(jnp.einsum('bld,ed->ble', x, w1) + b1)
            return jnp.tanh(jnp.einsum('bld,kd->blk', h, w2) + b2) * PI
        B, L, D = x.shape
        key_phase = _encode_phase(x, kw1, kb1, kw2, kb2)
        query_phase = _encode_phase(x, qw1, qb1, qw2, qb2)
        K = key_phase.shape[-1]
        value = jnp.einsum('bld,ed->ble', x, vw) + vb
        cos_k = jnp.cos(key_phase)[..., None]
        sin_k = jnp.sin(key_phase)[..., None]
        v_exp = value[:, :, None, :]
        mem_real = jnp.cumsum(cos_k * v_exp, axis=1)
        mem_imag = jnp.cumsum(sin_k * v_exp, axis=1)
        cos_q = jnp.cos(query_phase)[..., None]
        sin_q = jnp.sin(query_phase)[..., None]
        retrieved = jnp.sum(mem_real * cos_q + mem_imag * sin_q, axis=2)
        positions = jnp.arange(1, L + 1, dtype=x.dtype)
        norm = jnp.sqrt(positions * K)[None, :, None]
        return retrieved / norm

    def _L0_ffn_ref(x, W1, b1, Wg, bg, Wd, bd):
        import jax, jax.numpy as jnp
        import numpy as np
        C = 64
        HID = 256
        E = 8
        TEMP = 1.0
        orig_shape = x.shape
        xf = x.reshape(-1, orig_shape[-1])
        H = jax.nn.gelu(xf @ W1 + b1, approximate=False)
        probs = jax.nn.softmax((H @ Wg + bg) / TEMP, axis=-1)
        assign = jnp.argmax(probs, axis=-1)
        out = jnp.zeros_like(xf)
        for e in range(Wd.shape[0]):
            y = H @ Wd[e] + bd[e]
            sel = (assign == e)[:, None]
            out = out + jnp.where(sel, probs[:, e:e + 1] * y, 0.0)
        return out.reshape(orig_shape)
    h = _L0_tok_ref(x, L0_tok_emb, L0_tok_W, L0_tok_b)
    h = h + _L0_attn_ref(_layernorm(h, axis=-1), L0_attn_kw1, L0_attn_kb1, L0_attn_kw2, L0_attn_kb2, L0_attn_qw1, L0_attn_qb1, L0_attn_qw2, L0_attn_qb2, L0_attn_vw, L0_attn_vb)
    h = h + _L0_ffn_ref(_layernorm(h, axis=-1), L0_ffn_W1, L0_ffn_b1, L0_ffn_Wg, L0_ffn_bg, L0_ffn_Wd, L0_ffn_bd)
    return h

_drawn_inputs = setup_inputs


def setup_inputs(seed=0):
    import zlib

    import numpy as np

    out = dict(_drawn_inputs(seed))
    spreads = {'L0_attn_kb1': (0.0, 0.8),
     'L0_attn_kb2': (0.0, 0.1),
     'L0_attn_qb1': (0.0, 0.8),
     'L0_attn_qb2': (0.0, 0.1),
     'L0_attn_vb': (0.0, 0.1),
     'L0_ffn_b1': (0.0, 0.8),
     'L0_ffn_bg': (0.0, 0.8),
     'L0_ffn_bd': (0.0, 0.8)}
    factors = {'L0_attn_kw1': 6.85,
     'L0_attn_kw2': 8.0,
     'L0_attn_qw1': 8.0,
     'L0_attn_qw2': 8.0,
     'L0_ffn_W1': 8.0,
     'L0_ffn_Wg': 8.0,
     'L0_ffn_Wd': 8.0}
    for name, (base, spread) in spreads.items():
        noise = np.random.default_rng([zlib.crc32(name.encode()), seed]).standard_normal(out[name].shape)
        drawn = base * np.exp(spread * noise) if base else spread * noise
        out[name] = jnp.asarray(drawn.astype(out[name].dtype))
    for name, factor in factors.items():
        out[name] = (out[name] * factor).astype(out[name].dtype)
    return out
```

```python
import numpy as np
import concourse.bass as bass
from concourse import mybir
from contextlib import ExitStack

fp32 = mybir.dt.float32
fp32r = mybir.dt.float32r
int32 = mybir.dt.int32
ALU = mybir.AluOpType
ACT = mybir.ActivationFunctionType
AX = mybir.AxisListType.X

P = 128
BATCH, SEQ = 64, 256
D = 64
VOCAB, KSIZE = 50257, 9
REACH = KSIZE // 2
PHASES = 32
HIDDEN, EXPERTS = 256, 8
EPS = 1e-5

TOKENS = BATCH * SEQ
TILES = TOKENS // P
GT = 8
GROUPS = TILES // GT
HALF = GT // 2 * P
WINDOW = KSIZE * D
BLOCKS = (WINDOW + P - 1) // P
EDGE = 2 * REACH
LAST_START = VOCAB - KSIZE
WIN_COLS = WINDOW + 2 * EDGE + 1
TAIL = WIN_COLS - (BLOCKS - 1) * P
PI_BELOW = float(np.nextafter(np.float32(np.pi), np.float32(0)))

LAG_CONV, LAG_FEATURES, LAG_ATTEND, LAG_FFN = 0, 1, 2, 3
ITERATIONS = GROUPS + LAG_FFN

BANK_JOBS = {
    0: [("window0", 0), ("window2", 0), ("window4", 0), ("window6", 0), ("window8", 0)],
    1: [("window1", 0), ("window3", 0), ("window5", 0), ("window7", 0), ("window9", 0)],
    2: [("retrieved", 2), ("down_bias", 3), ("conv", 0)],
    3: [("retrieved_tok", 2), ("weights_ch", 3), ("conv_tok", 0)],
    4: [("ffn_in0", 3), ("attn_in0", 1), ("up0", 3), ("up2", 3), ("scores0", 2), ("scores2", 2),
        ("hidden0", 1), ("gate", 3), ("value0", 1), ("phase_k", 1)],
    5: [("ffn_in1", 3), ("attn_in1", 1), ("up1", 3), ("up3", 3), ("scores1", 2), ("scores3", 2),
        ("hidden1", 1), ("gate_tok", 3), ("value1", 1), ("phase_q", 1)],
    6: [("expert0", 3), ("expert2", 3), ("expert4", 3), ("expert6", 3)],
    7: [("expert1", 3), ("expert3", 3), ("expert5", 3), ("expert7", 3)],
}
BANK_OF = {job: bank for bank, jobs in BANK_JOBS.items() for job, _ in jobs}


def jobs_before(job, i, groups):
    jobs = BANK_JOBS[BANK_OF[job]]
    count, reached = 0, False
    for name, lag in jobs:
        reached = reached or name == job
        if isinstance(i, int):
            count += min(max(i - lag, 0), groups)
            if not reached and 0 <= i - lag < groups:
                count += 1
        else:
            count += -lag + (0 if reached else 1)
    return count if isinstance(i, int) else i * len(jobs) + count


class Chain:

    def __init__(self, engine, sem, group, steps):
        self.engine, self.sem, self.base, self.steps, self.n = engine, sem, group * steps, steps, 0

    def __call__(self, instruction):
        self.n += 1
        instruction.then_inc(self.sem, 1)
        self.engine.wait_ge(self.sem, self.base + self.n)

    def end(self):
        assert self.n == self.steps


def over_last(ap, n):
    return ap.unsqueeze(2).broadcast_to([ap.shape[0], ap.shape[1], n])


def build(nc, x, emb, conv_w, conv_b, kw1, kb1, kw2, kb2, qw1, qb1, qw2, qb2, vw, vb,
          w1, b1, wg, bg, wd, bd, out, groups=GROUPS):
    iterations = groups + LAG_FFN
    tiles = groups * GT
    with ExitStack() as ctx:
        def sb(name, shape, dt=fp32):
            return ctx.enter_context(nc.sbuf_tensor(name, shape, dt))

        def sem(name):
            return ctx.enter_context(nc.semaphore(name))

        ident = sb("ident", [P, P])
        mask = sb("mask", [P, 3 * P])
        norm = sb("norm", [P, 3 * P])
        priority = sb("priority", [P, EXPERTS])
        edge_ids = sb("edge_ids", [P, 2 * EDGE])
        conv_wt = sb("conv_wt", [P, BLOCKS, D])
        conv_rows = sb("conv_rows", [D, KSIZE, D])
        edge_rows = sb("edge_rows", [2 * (EDGE + KSIZE), D])
        edge_cols = sb("edge_cols", [D, 2 * (EDGE + KSIZE)])
        edge_diff = sb("edge_diff", [D, KSIZE, 2 * EDGE])
        kq_raw = sb("kq_raw", [P, P])
        kq_hi = sb("kq_hi", [P, P], fp32r)
        kq_lo = sb("kq_lo", [P, P], fp32r)
        v_raw = sb("v_raw", [P, 4 * D])
        v_hi = sb("v_hi", [P, 4 * D], fp32r)
        v_lo = sb("v_lo", [P, 4 * D], fp32r)
        up_raw = sb("up_raw", [P, HIDDEN])
        up_hi = sb("up_hi", [P, HIDDEN], fp32r)
        up_lo = sb("up_lo", [P, HIDDEN], fp32r)
        down_raw = sb("down_raw", [P, 2, EXPERTS * D])
        down_hi = sb("down_hi", [P, 2, EXPERTS * D], fp32r)
        down_lo = sb("down_lo", [P, 2, EXPERTS * D], fp32r)
        phase_k_w = sb("phase_k_w", [P, D])
        phase_q_w = sb("phase_q_w", [P, D])
        gate_w = sb("gate_w", [P, 2, D])
        down_b = sb("down_b", [GT * EXPERTS, GT * D])
        hidden_b = sb("hidden_b", [P, 1])
        phase_k_b = sb("phase_k_b", [P, 1])
        phase_q_b = sb("phase_q_b", [P, 1])
        v_b = sb("v_b", [P, D])
        up_b = sb("up_b", [P, 2])
        gate_b = sb("gate_b", [P, 1])
        fold = sb("fold", [P, 1])
        sin_scale = sb("sin_scale", [P, 1])
        sin_shift = sb("sin_shift", [P, 1])
        minus_half = sb("minus_half", [P, GT])

        x_rows = sb("x_rows", [P, P], int32)
        x_float = sb("x_float", [P, P])
        x_edge = sb("x_edge", [P, TILES])
        x_start_f = sb("x_start_f", [P, TILES])
        x_start = sb("x_start", [P, TILES], int32)
        start8 = sb("start8", [P, GT], int32)

        h_all = sb("h_all", [P, TILES, D])
        window = sb("window", [P, GT, WIN_COLS])
        window_t = sb("window_t", [P, BLOCKS, GT * P])
        conv_ch = sb("conv_ch", [P, HALF])
        sums = {s: sb(f"sums{s}", [P, GT]) for s in (1, 2)}
        neg_mean = {s: sb(f"neg_mean{s}", [P, GT]) for s in (1, 2)}
        variance = {s: sb(f"variance{s}", [P, GT]) for s in (1, 2)}
        rstd = {s: sb(f"rstd{s}", [P, GT]) for s in (1, 2)}
        centred = sb("centred", [P, GT, D])
        squares = sb("squares", [P, GT, D])
        normed = {s: sb(f"normed{s}", [P, GT, 2, D]) for s in (1, 2)}
        normed_t = {s: sb(f"normed_t{s}", [P, GT * P], fp32r) for s in (1, 2)}
        hidden = sb("hidden", [P, GT * P])
        turn = {s: sb(f"turn_{s}", [P, HALF]) for s in "kq"}
        folded = {s: sb(f"folded_{s}", [P, HALF]) for s in "kq"}
        feature = {s: sb(f"feature_{s}", [P, HALF]) for s in "kq"}
        value = sb("value", [P, GT, D])
        attn = sb("attn", [P, 4, 3 * P])
        retrieved = sb("retrieved", [P, HALF])
        act = sb("act", [P, 2, GT * P])
        act_hi = sb("act_hi", [P, 2, GT * P], fp32r)
        act_lo = sb("act_lo", [P, 2, GT * P], fp32r)
        logits_ch = sb("logits_ch", [P, HALF])
        top = sb("top", [P, GT])
        below = sb("below", [P, GT, EXPERTS])
        ranked = sb("ranked", [P, GT, EXPERTS])
        first = sb("first", [P, GT])
        chosen = sb("chosen", [P, GT, EXPERTS])
        exps = sb("exps", [P, GT, EXPERTS])
        total = sb("total", [P, GT])
        top_prob = sb("top_prob", [P, GT])
        weight = sb("weight", [P, 2 * GT, EXPERTS])
        weight_ch = sb("weight_ch", [GT * EXPERTS, P])
        picked = sb("picked", [P, GT, EXPERTS * D])
        add4 = sb("add4", [P, 2, 4 * D])
        add2 = sb("add2", [P, 2, 2 * D])
        expert_out = sb("expert_out", [P, GT, D])
        base = sb("base", [P, GT, D])
        result = sb("result", [P, GT, D])

        bank = [ctx.enter_context(nc.psum_tensor(f"bank{b}", [P, 512], fp32)) for b in range(8)]
        full = [sem(f"bank{b}_full") for b in range(8)]
        free = [sem(f"bank{b}_free") for b in range(8)]

        s_x = sem("s_x")
        s_conv_w = sem("s_conv_w")
        s_edge_rows = sem("s_edge_rows")
        s_loads = sem("s_loads")
        s_const = sem("s_const")
        s_row_const = sem("s_row_const")
        s_ident = sem("s_ident")
        s_zero = sem("s_zero")
        s_norm = sem("s_norm")
        s_sqrt = sem("s_sqrt")
        s_setup_pe = sem("s_setup_pe")
        s_x_float = sem("s_x_float")
        s_edge_cols = sem("s_edge_cols")
        s_edge_diff = sem("s_edge_diff")
        s_conv_ready = sem("s_conv_ready")
        s_weights_ready = sem("s_weights_ready")
        gathered = [sem(f"gathered{h}") for h in range(2)]
        gather_ready = sem("gather_ready")
        window_cols = sem("window_cols")
        rstd_ready = {s: sem(f"rstd_ready{s}") for s in (1, 2)}
        normed_ready = {s: sem(f"normed_ready{s}") for s in (1, 2)}
        folded_ready = sem("folded_ready")
        feature_ready = sem("feature_ready")
        split_hi = sem("split_hi")
        split_ready = sem("split_ready")
        expert_sum = sem("expert_sum")
        exps_ready = sem("exps_ready")
        weight_ready = sem("weight_ready")
        result_ready = sem("result_ready")
        stored = sem("stored")
        chain_ln = {s: sem(f"chain_ln{s}") for s in (1, 2)}
        chain_soft = sem("chain_soft")
        chain_adds = sem("chain_adds")
        chain_setup = sem("chain_setup")

        LN_STEPS, SOFT_STEPS, ADD_STEPS, SETUP_STEPS = 8, 6, 8, 10
        ZEROED, CONSTS_EARLY, CONSTS, LOADS = 6, 6, 8, 38

        block = ctx.enter_context(nc.Block())

        def emit(body):
            def program(eng):
                lead = LAG_FFN + 1
                for i in range(lead):
                    body(eng, i)
                if groups - 1 > lead:
                    with eng.Fori(lead, groups - 1) as i:
                        body(eng, i)
                for i in range(max(groups - 1, lead), iterations):
                    body(eng, i)
            return program

        def runs(i, lag):
            return not isinstance(i, int) or 0 <= i - lag < groups

        def wait_full(eng, job, i):
            eng.wait_ge(full[BANK_OF[job]], jobs_before(job, i, groups) + 1)

        def wait_free(eng, job, i):
            n = jobs_before(job, i, groups)
            if not isinstance(n, int) or n > 0:
                eng.wait_ge(free[BANK_OF[job]], n)

        def wait_taken(eng, job, i):
            eng.wait_ge(free[BANK_OF[job]], jobs_before(job, i, groups) + 1)

        def tiles_of(ap, g):
            return ap[:, bass.ds(g * GT, GT), :]

        def evacuate_window(eng, copy, n, i):
            half, k = divmod(n, BLOCKS)
            rows = P if k < BLOCKS - 1 else TAIL
            job = f"window{n}"
            wait_full(eng, job, i)
            copy(window_t[0:rows, k, half * HALF:(half + 1) * HALF], bank[BANK_OF[job]][0:rows, :])\
                .then_inc(free[BANK_OF[job]], 1)

        @block.sync
        def _(sp):
            n_rows = tiles
            sp.dma_start(x_rows[0:n_rows, :], x.rearrange("(t p) -> t p", p=P)[0:n_rows, :]).then_inc(s_x, 16)
            k = EDGE + KSIZE
            sp.dma_start(edge_rows[0:EDGE, :], emb[0:1, :].broadcast_to([EDGE, D])).then_inc(s_edge_rows, 16)
            sp.dma_start(edge_rows[EDGE:k, :], emb[0:KSIZE, :]).then_inc(s_edge_rows, 16)
            sp.dma_start(edge_rows[k:k + KSIZE, :], emb[LAST_START:VOCAB, :]).then_inc(s_edge_rows, 16)
            sp.dma_start(edge_rows[k + KSIZE:2 * k, :],
                         emb[VOCAB - 1:VOCAB, :].broadcast_to([EDGE, D])).then_inc(s_edge_rows, 16)
            whole = (BLOCKS - 1) * P
            sp.dma_start(conv_wt[:, 0:BLOCKS - 1, :],
                         conv_w[0:whole, :].rearrange("(k p) o -> p k o", p=P)).then_inc(s_conv_w, 16)
            sp.dma_start(conv_wt[0:D, BLOCKS - 1, :], conv_w[whole:WINDOW, :]).then_inc(s_conv_w, 16)
            sp.dma_start(conv_wt[TAIL - 1:TAIL, BLOCKS - 1, :],
                         conv_b.rearrange("(a o) -> a o", a=1)).then_inc(s_conv_w, 16)
            sp.dma_start(conv_rows[:, :, :], conv_w.rearrange("(k p) o -> p k o", p=D)).then_inc(s_conv_w, 16)

            sp.wait_ge(s_zero, ZEROED)
            loads = []
            for r in (0, D):
                loads += [(kq_raw[r:r + D, 0:D], kw1), (kq_raw[r:r + D, D:P], qw1), (v_raw[r:r + D, 0:D], vw), (up_raw[r:r + D, :], w1)]
            for c in (0, PHASES):
                loads += [(phase_k_w[0:D, c:c + PHASES], kw2), (phase_q_w[D:P, c:c + PHASES], qw2)]
            loads += [(gate_w[:, :, 0:EXPERTS], wg.rearrange("(k p) e -> p k e", p=P))]
            wd_v = wd.rearrange("e (k p) d -> k p e d", p=P)
            for c in range(2):
                loads += [(down_raw[:, c, :].rearrange("p (e d) -> p e d", e=EXPERTS), wd_v[c])]
            for t in range(GT):
                loads += [(down_b[t * EXPERTS:(t + 1) * EXPERTS, t * D:(t + 1) * D], bd)]

            def column(v):
                return v.rearrange("(p a) -> p a", a=1)

            loads += [(hidden_b[0:D, :], column(kb1)), (hidden_b[D:P, :], column(qb1)),
                      (v_b[:, :], vb.rearrange("(a d) -> a d", a=1).broadcast_to([P, D])),
                      (gate_b[0:EXPERTS, :], column(bg)), (gate_b[D:D + EXPERTS, :], column(bg)),
                      (up_b[:, 0:1], column(b1[0:P])), (up_b[:, 1:2], column(b1[P:HIDDEN]))]
            for r in range(0, P, PHASES):
                loads += [(phase_k_b[r:r + PHASES, :], column(kb2)), (phase_q_b[r:r + PHASES, :], column(qb2))]
            assert len(loads) == LOADS
            for dst, src in loads:
                sp.dma_start(dst, src).then_inc(s_loads, 16)

            def store(eng, i):
                if runs(i, LAG_FFN):
                    g = i - LAG_FFN
                    eng.wait_ge(result_ready, g + 1)
                    dst = out.rearrange("(t p) d -> p t d", p=P)[:, bass.ds(g * GT, GT), :]
                    eng.dma_start(dst, result[:, :, :]).then_inc(stored, 16)

            emit(store)(sp)
            sp.wait_ge(stored, 16 * groups)

        @block.gpsimd
        def _(pool):
            G = nc.gpsimd
            G.memset(ident[:, :], 0.0).then_inc(s_ident, 1)
            pool.wait_ge(s_ident, 1)
            G.affine_select(out=ident[:, :], in_=ident[:, :], compare_op=ALU.not_equal, fill=1.0, base=0,
                            pattern=[[-1, P]], channel_multiplier=1).then_inc(s_ident, 1)
            for tile in (v_raw, phase_k_w, phase_q_w, gate_w, gate_b, down_b):
                ap = tile[:, :, :] if len(tile.shape) == 3 else tile[:, :]
                G.memset(ap, 0.0).then_inc(s_zero, 1)
            G.iota(edge_ids[:, 0:EDGE], pattern=[[1, EDGE]], base=-REACH, channel_multiplier=0,
                   allow_small_or_imprecise_dtypes=True).then_inc(s_const, 1)
            G.iota(edge_ids[:, EDGE:2 * EDGE], pattern=[[1, EDGE]], base=VOCAB - REACH, channel_multiplier=0,
                   allow_small_or_imprecise_dtypes=True).then_inc(s_const, 1)
            G.iota(priority[:, :], pattern=[[-1, EXPERTS]], base=EXPERTS, channel_multiplier=0,
                   allow_small_or_imprecise_dtypes=True).then_inc(s_const, 1)
            G.memset(window[:, :, WIN_COLS - 1:WIN_COLS], 1.0).then_inc(s_const, 1)
            G.memset(minus_half[:, :], -0.5).then_inc(s_const, 1)
            G.memset(weight[:, :, :], 0.0).then_inc(s_const, 1)
            G.iota(norm[:, :], pattern=[[PHASES, 3 * P]], base=PHASES, channel_multiplier=0,
                   allow_small_or_imprecise_dtypes=True).then_inc(s_norm, 1)
            pool.wait_ge(s_norm, 1)
            G.iota(norm[:, 2 * P:3 * P], pattern=[[PHASES, P]], base=PHASES * (P + 1), channel_multiplier=0,
                   allow_small_or_imprecise_dtypes=True).then_inc(s_norm, 1)
            def gather(eng, g, half):
                for t in range(4 * half, 4 * half + 4):
                    eng.indirect_dma_start(
                        out=window[:, t, 0:WINDOW], out_offset=None, in_=emb,
                        in_offset=bass.IndirectOffsetOnAxis(ap=start8[:, t:t + 1], axis=0),
                    ).then_inc(gathered[half], 16)

            pool.wait_ge(gather_ready, 1)
            gather(pool, 0, 0)
            gather(pool, 0, 1)
            pool.wait_ge(s_norm, 3)
            G.affine_select(out=mask[:, 0:2 * P], in_=mask[:, 0:2 * P], compare_op=ALU.is_ge, fill=0.0, base=0,
                            pattern=[[1, 2 * P]], channel_multiplier=-1).then_inc(s_const, 1)
            G.affine_select(out=mask[:, 2 * P:3 * P], in_=mask[:, 2 * P:3 * P], compare_op=ALU.is_ge, fill=0.0,
                            base=0, pattern=[[1, P]], channel_multiplier=-1).then_inc(s_const, 1)

            def inverse_root(eng, s, g):
                eng.wait_ge(chain_ln[s], g * LN_STEPS + 6)
                G.tensor_tensor(rstd[s][:, :], variance[s][:, :], minus_half[:, :], ALU.pow)\
                    .then_inc(rstd_ready[s], 1)

            def body(eng, i):
                if runs(i, LAG_ATTEND):
                    inverse_root(eng, 2, i - LAG_ATTEND)
                ffn = runs(i, LAG_FFN)
                g = i - LAG_FFN
                chain = Chain(eng, chain_adds, g, ADD_STEPS)
                for pair in range(GT // 2):
                    more = pair in (1, 3) and runs(i + 1, LAG_CONV)

                    def wait_room():
                        if more and runs(i, LAG_CONV):
                            wait_full(eng, "window4" if pair == 1 else "window9", i)
                        if more:
                            eng.wait_ge(gather_ready, i + 2)

                    if ffn:
                        two = slice(2 * pair, 2 * pair + 2)
                        wait_taken(eng, f"expert{2 * pair + 1}", i)
                        chain(G.tensor_tensor(add4[:, :, :], picked[:, two, 0:4 * D],
                                              picked[:, two, 4 * D:8 * D], ALU.add))
                        chain(G.tensor_tensor(add2[:, :, :], add4[:, :, 0:2 * D], add4[:, :, 2 * D:4 * D],
                                              ALU.add))
                        wait_room()
                        last = G.tensor_tensor(expert_out[:, two, :], add2[:, :, 0:D], add2[:, :, D:2 * D],
                                               ALU.add)
                        if pair == GT // 2 - 1:
                            last.then_inc(expert_sum, 1)
                    else:
                        wait_room()
                    if more:
                        gather(eng, i + 1, pair // 2)
                if ffn:
                    chain.end()
                    eng.wait_ge(expert_sum, g + 1)
                    wait_taken(eng, "down_bias", i)
                    if not isinstance(g, int) or g > 0:
                        eng.wait_ge(stored, 16 * g)
                    G.tensor_tensor(result[:, :, :], expert_out[:, :, :], base[:, :, :], ALU.add)\
                        .then_inc(result_ready, 1)
                if runs(i, LAG_CONV):
                    inverse_root(eng, 1, i)

            emit(body)(pool)

        @block.scalar
        def _(sc):
            S = nc.scalar
            sc.wait_ge(s_norm, 2)
            S.activation(norm[:, :], norm[:, :], ACT.Sqrt).then_inc(s_sqrt, 1)
            sc.wait_ge(s_edge_cols, 1)
            S.activation(edge_cols[:, :], bank[7][0:D, 0:2 * (EDGE + KSIZE)], ACT.Copy).then_inc(s_edge_cols, 1)
            sc.wait_ge(s_loads, 16 * LOADS)
            sc.wait_ge(s_row_const, 12)

            def body(eng, i):
                if runs(i, LAG_FFN):
                    g = i - LAG_FFN
                    for half in range(2):
                        job = f"ffn_in{half}"
                        wait_full(eng, job, i)
                        S.activation(normed_t[2][:, half * HALF:(half + 1) * HALF], bank[BANK_OF[job]][:, :],
                                     ACT.Copy).then_inc(free[BANK_OF[job]], 1)
                if runs(i, LAG_FEATURES):
                    for half in range(2):
                        job = f"attn_in{half}"
                        wait_full(eng, job, i)
                        S.activation(normed_t[1][:, half * HALF:(half + 1) * HALF], bank[BANK_OF[job]][:, :],
                                     ACT.Copy).then_inc(free[BANK_OF[job]], 1)
                if runs(i, LAG_FFN):
                    for n in range(4):
                        half, part = divmod(n, 2)
                        job = f"up{n}"
                        wait_full(eng, job, i)
                        S.activation(act[:, part, half * HALF:(half + 1) * HALF], bank[BANK_OF[job]][:, :],
                                     ACT.Gelu, bias=up_b[:, part:part + 1]).then_inc(free[BANK_OF[job]], 1)
                if runs(i, LAG_FEATURES):
                    for half in range(2):
                        job = f"hidden{half}"
                        wait_full(eng, job, i)
                        S.activation(hidden[:, half * HALF:(half + 1) * HALF], bank[BANK_OF[job]][:, :],
                                     ACT.Tanh, bias=hidden_b[:, 0:1]).then_inc(free[BANK_OF[job]], 1)
                if runs(i, LAG_FFN):
                    wait_full(eng, "gate", i)
                    S.activation(logits_ch[:, :], bank[4][:, :], ACT.Identity, bias=gate_b[:, 0:1])\
                        .then_inc(free[4], 1)
                if runs(i, LAG_ATTEND):
                    wait_full(eng, "retrieved", i)
                    S.activation(retrieved[:, :], bank[2][:, :], ACT.Copy).then_inc(free[2], 1)
                if runs(i, LAG_FFN):
                    eng.wait_ge(chain_soft, g * SOFT_STEPS + 2)
                    S.activation(exps[:, :, :], below[:, :, :], ACT.Exp).then_inc(exps_ready, 1)
                for n in (0, 2, 4):
                    if runs(i, LAG_CONV):
                        evacuate_window(eng, S.copy, n, i)
                if runs(i, LAG_FFN):
                    wait_full(eng, "weights_ch", i)
                    S.activation(weight_ch[:, :], bank[3][0:GT * EXPERTS, 0:P], ACT.Copy).then_inc(free[3], 1)
                for n in (6, 8):
                    if runs(i, LAG_CONV):
                        evacuate_window(eng, S.copy, n, i)
                if runs(i, LAG_FEATURES):
                    g = i - LAG_FEATURES
                    for s, bias in (("k", phase_k_b), ("q", phase_q_b)):
                        job = f"phase_{s}"
                        wait_full(eng, job, i)
                        S.activation(turn[s][:, :], bank[BANK_OF[job]][:, :], ACT.Tanh, bias=bias[:, 0:1])\
                            .then_inc(free[BANK_OF[job]], 1)
                if runs(i, LAG_CONV):
                    wait_full(eng, "conv", i)
                    S.activation(conv_ch[:, :], bank[2][:, :], ACT.Copy).then_inc(free[2], 1)
                if runs(i, LAG_FEATURES):
                    for n, s in enumerate("kq"):
                        eng.wait_ge(folded_ready, 2 * g + n + 1)
                        S.activation(feature[s][:, :], folded[s][:, :], ACT.Sin, scale=sin_scale[:, 0:1],
                                     bias=sin_shift[:, 0:1]).then_inc(feature_ready, 1)

            emit(body)(sc)

        @block.vector
        def _(dve):
            V = nc.vector
            link = Chain(dve, chain_setup, 0, SETUP_STEPS)
            for q in range(4):
                rows = slice(32 * q, 32 * q + 32)
                cosine = q % 2 == 0
                V.memset(fold[rows, :], -1.0 if cosine else 1.0).then_inc(s_row_const, 1)
                V.memset(sin_scale[rows, :], -PI_BELOW if cosine else PI_BELOW).then_inc(s_row_const, 1)
                V.memset(sin_shift[rows, :], float(np.pi / 2) if cosine else 0.0).then_inc(s_row_const, 1)
            dve.wait_ge(s_x, 16)
            V.tensor_copy(x_float[0:tiles, :], x_rows[0:tiles, :]).then_inc(s_x_float, 1)
            dve.wait_ge(s_x_float, 1)
            link(V.tensor_scalar(x_float[0:tiles, :], x_float[0:tiles, :], float(-REACH),
                                 float(VOCAB + REACH - 1), ALU.max, ALU.min))
            dve.wait_ge(s_setup_pe, 1)
            link(V.tensor_copy(x_edge[:, 0:tiles], bank[6][:, 0:tiles]))
            link(V.tensor_scalar(x_start_f[:, 0:tiles], x_edge[:, 0:tiles], float(-REACH), 0.0, ALU.add, ALU.max))
            link(V.tensor_scalar(x_start_f[:, 0:tiles], x_start_f[:, 0:tiles], float(LAST_START), None, ALU.min))
            link(V.tensor_copy(x_start[:, 0:tiles], x_start_f[:, 0:tiles]))

            def prepare_window(eng, g):
                V.tensor_copy(start8[:, :], x_start[:, bass.ds(g * GT, GT)]).then_inc(gather_ready, 1)
                if isinstance(g, int) and g == 0:
                    eng.wait_ge(s_const, CONSTS_EARLY)
                V.tensor_tensor(window[:, :, WINDOW:WINDOW + 2 * EDGE],
                                over_last(x_edge[:, bass.ds(g * GT, GT)], 2 * EDGE),
                                edge_ids[:, :].unsqueeze(1).broadcast_to([P, GT, 2 * EDGE]),
                                ALU.is_equal).then_inc(window_cols, 1)

            prepare_window(dve, 0)
            dve.wait_ge(s_sqrt, 1)
            V.reciprocal(mask[:, :], norm[:, :]).then_inc(s_norm, 1)
            dve.wait_ge(s_edge_cols, 2)
            k = EDGE + KSIZE
            for j in range(KSIZE):
                V.tensor_tensor(edge_diff[:, j, 0:EDGE], edge_cols[:, j:j + EDGE],
                                edge_cols[:, EDGE + j:EDGE + j + 1].broadcast_to([D, EDGE]),
                                ALU.subtract).then_inc(s_edge_diff, 1)
                V.tensor_tensor(edge_diff[:, j, EDGE:2 * EDGE], edge_cols[:, k + 1 + j:k + 1 + j + EDGE],
                                edge_cols[:, k + j:k + j + 1].broadcast_to([D, EDGE]),
                                ALU.subtract).then_inc(s_edge_diff, 1)
            dve.wait_ge(s_setup_pe, 3)
            V.tensor_copy(conv_wt[D:D + 2 * EDGE, BLOCKS - 1, :], bank[6][D:D + 2 * EDGE, 0:D])\
                .then_inc(s_conv_ready, 1)
            dve.wait_ge(s_loads, 16 * LOADS)
            for raw, hi, lo in ((kq_raw, kq_hi, kq_lo), (v_raw, v_hi, v_lo), (up_raw, up_hi, up_lo)):
                link(V.tensor_copy(hi[:, :], raw[:, :]))
                V.tensor_tensor(lo[:, :], raw[:, :], hi[:, :].bitcast(fp32), ALU.subtract)\
                    .then_inc(s_weights_ready, 1)
            for c in range(2):
                link(V.tensor_copy(down_hi[:, c, :], down_raw[:, c, :]))
                V.tensor_tensor(down_lo[:, c, :], down_raw[:, c, :], down_hi[:, c, :].bitcast(fp32),
                                ALU.subtract).then_inc(s_weights_ready, 1)
            link.end()
            dve.wait_ge(s_const, CONSTS)
            dve.wait_ge(s_row_const, 12)

            def layer_norm(eng, s, g):
                chain = Chain(eng, chain_ln[s], g, LN_STEPS)
                h = tiles_of(h_all, g)
                chain(V.tensor_reduce(sums[s][:, :], h, axis=AX, op=ALU.add))
                chain(V.tensor_scalar(neg_mean[s][:, :], sums[s][:, :], -1.0 / D, None, ALU.mult))
                chain(V.tensor_tensor(centred[:, :, :], h, over_last(neg_mean[s][:, :], D), ALU.add))
                chain(V.tensor_tensor(squares[:, :, :], centred[:, :, :], centred[:, :, :], ALU.mult))
                chain(V.tensor_reduce(sums[s][:, :], squares[:, :, :], axis=AX, op=ALU.add))
                chain(V.tensor_scalar(variance[s][:, :], sums[s][:, :], 1.0 / D, EPS, ALU.mult, ALU.add))
                eng.wait_ge(rstd_ready[s], g + 1)
                chain(V.tensor_tensor(squares[:, :, :], centred[:, :, :], over_last(rstd[s][:, :], D), ALU.mult))
                hi, lo = normed[s][:, :, 0, :], normed[s][:, :, 1, :]
                chain(V.tensor_copy(hi.bitcast(fp32r), squares[:, :, :]))
                V.tensor_tensor(lo, squares[:, :, :], hi, ALU.subtract).then_inc(normed_ready[s], 1)
                chain.end()

            def by_half(b):
                return bank[b][:, :].rearrange("p (s h d) -> p h s d", h=2, d=D)

            def expert(eng, t, i):
                job = f"expert{t}"
                g = i - LAG_FFN
                if t == 0:
                    eng.wait_ge(weight_ready, g + 1)
                    if not isinstance(g, int) or g > 0:
                        eng.wait_ge(expert_sum, g)
                wait_full(eng, job, i)
                V.tensor_tensor(picked[:, t, :].rearrange("p (e d) -> p e d", e=EXPERTS),
                                bank[BANK_OF[job]][:, :].rearrange("p (e d) -> p e d", e=EXPERTS),
                                over_last(weight[:, t, :], D), ALU.mult).then_inc(free[BANK_OF[job]], 1)

            def body(eng, i):
                conv, features, attend, ffn = (runs(i, lag) for lag in
                                               (LAG_CONV, LAG_FEATURES, LAG_ATTEND, LAG_FFN))
                if attend:
                    for n in range(4):
                        job = f"scores{n}"
                        wait_full(eng, job, i)
                        V.tensor_tensor(attn[:, n, :], bank[BANK_OF[job]][:, 0:3 * P], mask[:, :], ALU.mult)\
                            .then_inc(free[BANK_OF[job]], 1)
                if ffn:
                    for n in range(4):
                        half, part = divmod(n, 2)
                        cols = slice(half * HALF, (half + 1) * HALF)
                        wait_taken(eng, f"up{n}", i)
                        V.tensor_copy(act_hi[:, part, cols], act[:, part, cols]).then_inc(split_hi, 1)
                        eng.wait_ge(split_hi, (i - LAG_FFN) * 4 + n + 1)
                        V.tensor_tensor(act_lo[:, part, cols], act[:, part, cols],
                                        act_hi[:, part, cols].bitcast(fp32), ALU.subtract).then_inc(split_ready, 1)
                    g = i - LAG_FFN
                    wait_full(eng, "gate_tok", i)
                    chain = Chain(eng, chain_soft, g, SOFT_STEPS)
                    logits = by_half(5)[:, :, :, 0:EXPERTS]
                    chain(V.tensor_reduce(top[:, :].rearrange("p (h s) -> p h s", h=2), logits, axis=AX, op=ALU.max))
                    chain(V.tensor_tensor(
                        below[:, :, :].rearrange("p (h s) e -> p h s e", h=2), logits,
                        top[:, :].rearrange("p (h s) -> p h s", h=2).unsqueeze(3)
                        .broadcast_to([P, 2, 4, EXPERTS]), ALU.subtract))
                    V.scalar_tensor_tensor(ranked[:, :, :], below[:, :, :], 0.0,
                                           priority[:, :].unsqueeze(1).broadcast_to([P, GT, EXPERTS]),
                                           ALU.is_equal, ALU.mult).then_inc(free[5], 1)
                    wait_taken(eng, "gate_tok", i)
                    chain(V.tensor_reduce(first[:, :], ranked[:, :, :], axis=AX, op=ALU.max))
                    chain(V.tensor_tensor(chosen[:, :, :], ranked[:, :, :], over_last(first[:, :], EXPERTS),
                                          ALU.is_equal))
                    eng.wait_ge(exps_ready, g + 1)
                    chain(V.tensor_reduce(total[:, :], exps[:, :, :], axis=AX, op=ALU.add))
                    chain(V.reciprocal(top_prob[:, :], total[:, :]))
                    V.tensor_tensor(weight[:, 0:GT, :], chosen[:, :, :], over_last(top_prob[:, :], EXPERTS),
                                    ALU.mult).then_inc(weight_ready, 1)
                    chain.end()
                if attend:
                    g = i - LAG_ATTEND
                    wait_full(eng, "retrieved_tok", i)
                    h = tiles_of(h_all, g).rearrange("p (h s) d -> p h s d", h=2)
                    V.tensor_tensor(h, h, by_half(3), ALU.add).then_inc(free[3], 1)
                    wait_taken(eng, "retrieved_tok", i)
                if features:
                    for n in range(2):
                        job = f"value{n}"
                        wait_full(eng, job, i)
                        V.tensor_tensor(value[:, 4 * n:4 * n + 4, :],
                                        bank[BANK_OF[job]][:, 0:4 * D].rearrange("p (t d) -> p t d", t=4),
                                        v_b[:, :].unsqueeze(1).broadcast_to([P, 4, D]), ALU.add)\
                            .then_inc(free[BANK_OF[job]], 1)
                if attend:
                    layer_norm(eng, 2, i - LAG_ATTEND)
                for n in (1, 3, 5, 7, 9):
                    if conv:
                        evacuate_window(eng, V.tensor_copy, n, i)
                        if n == 9 and runs(i + 1, LAG_CONV):
                            prepare_window(eng, i + 1)
                    if ffn and n >= 3:
                        expert(eng, (n - 3) // 2, i)
                if features:
                    for n, s in enumerate("kq"):
                        wait_taken(eng, f"phase_{s}", i)
                        V.scalar_tensor_tensor(folded[s][:, :], turn[s][:, :], fold[:, 0:1], turn[s][:, :],
                                               ALU.mult, ALU.max).then_inc(folded_ready, 1)
                if ffn:
                    expert(eng, 4, i)
                    g = i - LAG_FFN
                    wait_full(eng, "down_bias", i)
                    if not isinstance(g, int) or g > 0:
                        eng.wait_ge(result_ready, g)
                    V.tensor_tensor(base[:, :, :], tiles_of(h_all, g),
                                    bank[2][:, :].rearrange("p (t d) -> p t d", t=GT), ALU.add)\
                        .then_inc(free[2], 1)
                    expert(eng, 5, i)
                if conv:
                    wait_full(eng, "conv_tok", i)
                    V.tensor_copy(tiles_of(h_all, i).rearrange("p (h s) d -> p h s d", h=2), by_half(3))\
                        .then_inc(free[3], 1)
                if ffn:
                    expert(eng, 6, i)
                if conv:
                    wait_taken(eng, "conv_tok", i)
                if ffn:
                    expert(eng, 7, i)
                if conv:
                    layer_norm(eng, 1, i)

            emit(body)(dve)

        @block.tensor
        def _(pe):
            T = nc.tensor
            pe.wait_ge(s_ident, 2)
            pe.wait_ge(chain_setup, 1)
            T.transpose(bank[6][:, 0:tiles], x_float[0:tiles, :], ident[0:tiles, 0:tiles]).then_inc(s_setup_pe, 1)
            k = 2 * (EDGE + KSIZE)
            pe.wait_ge(s_edge_rows, 64)
            T.transpose(bank[7][0:D, 0:k], edge_rows[:, :], ident[0:k, 0:k]).then_inc(s_edge_cols, 1)
            pe.wait_ge(s_conv_w, 64)
            pe.wait_ge(s_edge_diff, 2 * KSIZE)
            pe.wait_ge(chain_setup, 2)
            for j in range(KSIZE):
                last = T.matmul(bank[6][D:D + 2 * EDGE, 0:D], edge_diff[:, j, :], conv_rows[:, j, :],
                                start=(j == 0), stop=(j == KSIZE - 1))
            last.then_inc(s_setup_pe, 2)

            def token_to_channel(src, job, i):
                half = int(job[-1])
                wait_free(pe, job, i)
                for s in range(4):
                    last = T.transpose(bank[BANK_OF[job]][:, s * P:(s + 1) * P],
                                       src[:, 4 * half + s, :, :].rearrange("p a d -> p (a d)"), ident[:, :])
                last.then_inc(full[BANK_OF[job]], 1)

            def channel_to_token(src, job, i):
                wait_free(pe, job, i)
                for s in range(4):
                    last = T.transpose(bank[BANK_OF[job]][:, s * P:(s + 1) * P], src[:, s * P:(s + 1) * P],
                                       ident[:, :])
                last.then_inc(full[BANK_OF[job]], 1)

            def window_transpose(n, i):
                half, k = divmod(n, BLOCKS)
                if k == 0:
                    pe.wait_ge(gathered[half], 64 * (i + 1))
                if n == 4:
                    pe.wait_ge(window_cols, i + 1)
                job = f"window{n}"
                cols = slice(k * P, min((k + 1) * P, WIN_COLS))
                rows = cols.stop - cols.start
                wait_free(pe, job, i)
                for s in range(4):
                    last = T.transpose(bank[BANK_OF[job]][0:rows, s * P:(s + 1) * P],
                                       window[:, 4 * half + s, cols], ident[:, :])
                last.then_inc(full[BANK_OF[job]], 1)

            def by_halves(job, weights, src, i, k_rows=(P,)):
                b = BANK_OF[job]
                wait_free(pe, job, i)
                for k, rows in enumerate(k_rows):
                    for half in range(2):
                        last = T.matmul(bank[b][half * D:(half + 1) * D, :], weights(k)[0:rows, :],
                                        src(k)[0:rows, half * HALF:(half + 1) * HALF],
                                        start=(k == 0), stop=(k == len(k_rows) - 1))
                last.then_inc(full[b], 1)

            def two_parts(out_ap, hi, lo, src):
                T.matmul(out_ap, hi, src, start=True, stop=False)
                return T.matmul(out_ap, lo, src, start=False, stop=True)

            def expert(t, i):
                job = f"expert{t}"
                b = BANK_OF[job]
                pe.wait_ge(split_ready, (i - LAG_FFN) * 4 + (2 if t < 4 else 4))
                wait_free(pe, job, i)
                cols = slice(t * P, (t + 1) * P)
                products = [(act_hi, down_hi), (act_hi, down_lo), (act_lo, down_hi)]
                for k in range(2):
                    for n, (a, w) in enumerate(products):
                        last = T.matmul(bank[b][:, :], a[:, k, cols], w[:, k, :],
                                        start=(k == 0 and n == 0), stop=(k == 1 and n == 2))
                last.then_inc(full[b], 1)

            def body(eng, i):
                conv, features, attend, ffn = (runs(i, lag) for lag in
                                               (LAG_CONV, LAG_FEATURES, LAG_ATTEND, LAG_FFN))
                if ffn:
                    g = i - LAG_FFN
                    eng.wait_ge(normed_ready[2], g + 1)
                    token_to_channel(normed[2], "ffn_in0", i)
                    token_to_channel(normed[2], "ffn_in1", i)
                if features:
                    g = i - LAG_FEATURES
                    if isinstance(g, int) and g == 0:
                        eng.wait_ge(s_weights_ready, 5)
                        eng.wait_ge(s_loads, 16 * LOADS)
                    eng.wait_ge(normed_ready[1], g + 1)
                    token_to_channel(normed[1], "attn_in0", i)
                    token_to_channel(normed[1], "attn_in1", i)
                if ffn:
                    for n in range(4):
                        half, part = divmod(n, 2)
                        job = f"up{n}"
                        wait_taken(eng, f"ffn_in{half}", i)
                        wait_free(eng, job, i)
                        cols = slice(part * P, (part + 1) * P)
                        two_parts(bank[BANK_OF[job]][:, :], up_hi[:, cols], up_lo[:, cols],
                                  normed_t[2][:, half * HALF:(half + 1) * HALF])\
                            .then_inc(full[BANK_OF[job]], 1)
                if attend:
                    g = i - LAG_ATTEND
                    eng.wait_ge(feature_ready, 2 * g + 2)
                    for n in range(4):
                        half, seq = divmod(n, 2)
                        rows = slice(half * D, (half + 1) * D)
                        c = seq * SEQ
                        job = f"scores{n}"
                        b = BANK_OF[job]
                        wait_free(eng, job, i)
                        T.matmul(bank[b][:, 0:SEQ], feature["k"][rows, c:c + P], feature["q"][rows, c:c + SEQ],
                                 start=True, stop=True)
                        T.matmul(bank[b][:, SEQ:SEQ + P], feature["k"][rows, c + P:c + SEQ],
                                 feature["q"][rows, c + P:c + SEQ], start=True, stop=True)\
                            .then_inc(full[b], 1)
                if features:
                    for half in range(2):
                        job = f"hidden{half}"
                        wait_taken(eng, f"attn_in{half}", i)
                        wait_free(eng, job, i)
                        two_parts(bank[BANK_OF[job]][:, :], kq_hi[:, :], kq_lo[:, :],
                                  normed_t[1][:, half * HALF:(half + 1) * HALF])\
                            .then_inc(full[BANK_OF[job]], 1)
                if ffn:
                    wait_taken(eng, "up3", i)
                    by_halves("gate", lambda k: gate_w[:, k, :], lambda k: act[:, k, :], i, (P, P))
                if attend:
                    wait_free(eng, "retrieved", i)
                    for seq in range(2):
                        wait_taken(eng, f"scores{2 + seq}", i)
                        for part in range(2):
                            for half in range(2):
                                last = T.matmul(
                                    bank[2][half * D:(half + 1) * D, seq * SEQ + part * P:(seq + 1) * SEQ],
                                    value[:, 4 * half + 2 * seq + part, :],
                                    attn[:, 2 * half + seq, (0 if part == 0 else SEQ):SEQ + part * P],
                                    start=(part == 0), stop=(part == 1), skip_group_check=True)
                    last.then_inc(full[2], 1)
                if ffn:
                    wait_taken(eng, "gate", i)
                    channel_to_token(logits_ch, "gate_tok", i)
                if attend:
                    wait_taken(eng, "retrieved", i)
                    channel_to_token(retrieved, "retrieved_tok", i)
                if features:
                    for half in range(2):
                        job = f"value{half}"
                        b = BANK_OF[job]
                        wait_free(eng, job, i)
                        for s in range(4):
                            cols = slice((4 * half + s) * P, (4 * half + s + 1) * P)
                            out_ap = bank[b][:, s * D:(s + 4) * D]
                            T.matmul(out_ap, normed_t[1][:, cols], v_hi[:, :], start=True, stop=False)
                            last = T.matmul(out_ap, normed_t[1][:, cols], v_lo[:, :], start=False, stop=True)
                        last.then_inc(full[b], 1)
                if conv:
                    for n in (0, 1, 2):
                        window_transpose(n, i)
                if ffn:
                    expert(0, i)
                if conv:
                    for n in (3, 4, 5):
                        window_transpose(n, i)
                if ffn:
                    expert(1, i)
                    eng.wait_ge(weight_ready, i - LAG_FFN + 1)
                    wait_free(eng, "weights_ch", i)
                    T.transpose(bank[3][:, 0:P], weight[:, :, :].rearrange("p t e -> p (t e)"),
                                ident[:, :]).then_inc(full[3], 1)
                if conv:
                    for n in (6, 7):
                        window_transpose(n, i)
                if ffn:
                    expert(2, i)
                if conv:
                    for n in (8, 9):
                        window_transpose(n, i)
                if ffn:
                    expert(3, i)
                    wait_taken(eng, "weights_ch", i)
                    wait_free(eng, "down_bias", i)
                    T.matmul(bank[2][:, :], weight_ch[:, :], down_b[:, :], start=True, stop=True)\
                        .then_inc(full[2], 1)
                if features:
                    wait_taken(eng, "hidden1", i)
                    by_halves("phase_k", lambda k: phase_k_w[:, :], lambda k: hidden[:, :], i)
                    by_halves("phase_q", lambda k: phase_q_w[:, :], lambda k: hidden[:, :], i)
                if ffn:
                    expert(4, i)
                if conv:
                    if isinstance(i, int) and i == 0:
                        eng.wait_ge(s_conv_ready, 1)
                    wait_taken(eng, "window8", i)
                    wait_taken(eng, "window9", i)
                    by_halves("conv", lambda k: conv_wt[:, k, :], lambda k: window_t[:, k, :], i,
                              (P,) * (BLOCKS - 1) + (TAIL,))
                if ffn:
                    expert(5, i)
                if conv:
                    wait_taken(eng, "conv", i)
                    channel_to_token(conv_ch, "conv_tok", i)
                if ffn:
                    expert(6, i)
                    expert(7, i)

            emit(body)(pe)

    return nc


def kernel(**inputs):
    import numpy as _np
    import concourse.bacc as _bacc
    from concourse import mybir as _mybir
    from concourse.bass_utils import run_bass_kernel_spmd as _run

    def t(name):
        return _np.ascontiguousarray(_np.transpose(_np.asarray(inputs[name])))

    def plain(name):
        return _np.ascontiguousarray(_np.asarray(inputs[name]))

    conv_w = _np.asarray(inputs["L0_tok_W"])
    arrays = {
        "x": plain("x").reshape(-1),
        "emb": plain("L0_tok_emb"),
        "conv_w": _np.ascontiguousarray(_np.transpose(conv_w, (2, 1, 0))).reshape(WINDOW, D),
        "conv_b": plain("L0_tok_b"),
        "kw1": t("L0_attn_kw1"), "kb1": plain("L0_attn_kb1"), "kw2": t("L0_attn_kw2"), "kb2": plain("L0_attn_kb2"),
        "qw1": t("L0_attn_qw1"), "qb1": plain("L0_attn_qb1"), "qw2": t("L0_attn_qw2"), "qb2": plain("L0_attn_qb2"),
        "vw": t("L0_attn_vw"), "vb": plain("L0_attn_vb"),
        "w1": plain("L0_ffn_W1"), "b1": plain("L0_ffn_b1"), "wg": plain("L0_ffn_Wg"), "bg": plain("L0_ffn_bg"),
        "wd": plain("L0_ffn_Wd"), "bd": plain("L0_ffn_bd"),
    }
    nc = _bacc.Bacc("TRN2", target_bir_lowering=False, num_devices=1)
    args = [nc.dram_tensor(f"in_{n}", a.shape, _mybir.dt.from_np(a.dtype), kind="ExternalInput").ap()
            for n, a in arrays.items()]
    out = nc.dram_tensor("out_h", (TOKENS, D), _mybir.dt.float32, kind="ExternalOutput").ap()
    build(nc, *args, out)
    r = _run(nc, [{f"in_{n}": a for n, a in arrays.items()}], core_ids=[0])
    return r.results[0]["out_h"].reshape(BATCH, SEQ, D)
```

```python
import numpy as np
import concourse.bass as bass
from concourse import mybir
from contextlib import ExitStack

fp32 = mybir.dt.float32
fp32r = mybir.dt.float32r
int32 = mybir.dt.int32
ALU = mybir.AluOpType
ACT = mybir.ActivationFunctionType
AX = mybir.AxisListType.X

P = 128
BATCH, SEQ = 64, 256
D = 64
VOCAB, KSIZE = 50257, 9
REACH = KSIZE // 2
PHASES = 32
HIDDEN, EXPERTS = 256, 8
EPS = 1e-5

TOKENS = BATCH * SEQ
TILES = TOKENS // P
GT = 8
GROUPS = TILES // GT
HALF = GT // 2 * P
WINDOW = KSIZE * D
BLOCKS = (WINDOW + P - 1) // P
EDGE = 2 * REACH
LAST_START = VOCAB - KSIZE
WIN_COLS = WINDOW + 2 * EDGE + 1
TAIL = WIN_COLS - (BLOCKS - 1) * P
PI_BELOW = float(np.nextafter(np.float32(np.pi), np.float32(0)))

LAG_CONV, LAG_FEATURES, LAG_ATTEND, LAG_FFN = 0, 1, 2, 3
ITERATIONS = GROUPS + LAG_FFN

BANK_JOBS = {
    0: [("window0", 0), ("window2", 0), ("window4", 0), ("window6", 0), ("window8", 0)],
    1: [("window1", 0), ("window3", 0), ("window5", 0), ("window7", 0), ("window9", 0)],
    2: [("retrieved", 2), ("down_bias", 3), ("conv", 0)],
    3: [("retrieved_tok", 2), ("weights_ch", 3), ("conv_tok", 0)],
    4: [("ffn_in0", 3), ("up0", 3), ("up2", 3), ("attn_in0", 1), ("hidden0", 1), ("gate", 3), ("value0", 1),
        ("phase_k", 1)],
    5: [("ffn_in1", 3), ("up1", 3), ("up3", 3), ("attn_in1", 1), ("hidden1", 1), ("gate_tok", 3), ("value1", 1),
        ("phase_q", 1)],
    6: [("scores0_early", 2), ("scores1_early", 2), ("expert0", 3), ("expert2", 3), ("expert4", 3), ("expert6", 3)],
    7: [("scores0_late", 2), ("scores1_late", 2), ("expert1", 3), ("expert3", 3), ("expert5", 3), ("expert7", 3)],
}
BANK_OF = {job: bank for bank, jobs in BANK_JOBS.items() for job, _ in jobs}


def jobs_before(job, i, groups):
    jobs = BANK_JOBS[BANK_OF[job]]
    count, reached = 0, False
    for name, lag in jobs:
        reached = reached or name == job
        if isinstance(i, int):
            count += min(max(i - lag, 0), groups)
            if not reached and 0 <= i - lag < groups:
                count += 1
        else:
            count += -lag + (0 if reached else 1)
    return count if isinstance(i, int) else i * len(jobs) + count


class Chain:

    def __init__(self, engine, sem, group, steps, done=0):
        self.engine, self.sem, self.base, self.steps, self.n = engine, sem, group * steps, steps, done

    def __call__(self, instruction):
        self.n += 1
        instruction.then_inc(self.sem, 1)
        self.engine.wait_ge(self.sem, self.base + self.n)

    def end(self):
        assert self.n == self.steps


def over_last(ap, n):
    return ap.unsqueeze(2).broadcast_to([ap.shape[0], ap.shape[1], n])


def build(nc, x, emb, conv_w, conv_b, kw1, kb1, kw2, kb2, qw1, qb1, qw2, qb2, vw, vb,
          w1, b1, wg, bg, wd, bd, out, groups=GROUPS):
    iterations = groups + LAG_FFN
    tiles = groups * GT
    with ExitStack() as ctx:
        def sb(name, shape, dt=fp32):
            return ctx.enter_context(nc.sbuf_tensor(name, shape, dt))

        def sem(name):
            return ctx.enter_context(nc.semaphore(name))

        ident = sb("ident", [P, P])
        mask = sb("mask", [P, 3 * P])
        norm = sb("norm", [P, 3 * P])
        priority = sb("priority", [P, EXPERTS])
        edge_ids = sb("edge_ids", [P, 2 * EDGE])
        conv_wt = sb("conv_wt", [P, BLOCKS, D])
        conv_rows = sb("conv_rows", [D, KSIZE, D])
        edge_rows = sb("edge_rows", [2 * (EDGE + KSIZE), D])
        edge_cols = sb("edge_cols", [D, 2 * (EDGE + KSIZE)])
        edge_diff = sb("edge_diff", [D, KSIZE, 2 * EDGE])
        kq_raw = sb("kq_raw", [P, P])
        kq_hi = sb("kq_hi", [P, P], fp32r)
        kq_lo = sb("kq_lo", [P, P], fp32r)
        v_raw = sb("v_raw", [P, 3 * D])
        v_parts = sb("v_parts", [P, 4 * D], fp32r)
        up_raw = sb("up_raw", [P, HIDDEN])
        up_hi = sb("up_hi", [P, HIDDEN], fp32r)
        up_lo = sb("up_lo", [P, HIDDEN], fp32r)
        down_hi = sb("down_hi", [P, 2, EXPERTS * D], fp32r)
        down_lo = sb("down_lo", [P, 2, EXPERTS * D], fp32r)
        phase_k_w = sb("phase_k_w", [P, D])
        phase_q_w = sb("phase_q_w", [P, D])
        gate_w = sb("gate_w", [P, 2, D])
        down_b = sb("down_b", [GT * EXPERTS, GT * D])
        hidden_b = sb("hidden_b", [P, 1])
        phase_k_b = sb("phase_k_b", [P, 1])
        phase_q_b = sb("phase_q_b", [P, 1])
        v_b = sb("v_b", [P, D])
        up_b = sb("up_b", [P, 2])
        gate_b = sb("gate_b", [P, 1])
        fold = sb("fold", [P, 1])
        sin_scale = sb("sin_scale", [P, 1])
        sin_shift = sb("sin_shift", [P, 1])
        minus_half = sb("minus_half", [P, GT])

        x_rows = sb("x_rows", [P, P], int32)
        x_float = sb("x_float", [P, P])
        x_edge = sb("x_edge", [P, TILES])
        x_start_f = sb("x_start_f", [P, TILES])
        x_start = sb("x_start", [P, TILES], int32)
        start8 = sb("start8", [P, GT], int32)

        h_all = sb("h_all", [P, TILES, D])
        window = sb("window", [P, GT, WIN_COLS])
        window_t = sb("window_t", [P, BLOCKS, GT * P])
        conv_ch = sb("conv_ch", [P, HALF])
        sums = {s: sb(f"sums{s}", [P, GT]) for s in (1, 2)}
        neg_mean = {s: sb(f"neg_mean{s}", [P, GT]) for s in (1, 2)}
        variance = {s: sb(f"variance{s}", [P, GT]) for s in (1, 2)}
        rstd = {s: sb(f"rstd{s}", [P, GT]) for s in (1, 2)}
        centred = {s: sb(f"centred{s}", [P, GT, D]) for s in (1, 2)}
        squares = sb("squares", [P, GT, D])
        normed = {s: sb(f"normed{s}", [P, GT, 2, D]) for s in (1, 2)}
        normed_t = {s: sb(f"normed_t{s}", [P, GT * P], fp32r) for s in (1, 2)}
        hidden = sb("hidden", [P, GT * P])
        turn = {s: sb(f"turn_{s}", [P, HALF]) for s in "kq"}
        folded = {s: sb(f"folded_{s}", [P, HALF]) for s in "kq"}
        feature_k = sb("feature_k", [P, HALF])
        feature_q = sb("feature_q", [P, 2, HALF])
        value_hi = sb("value_hi", [P, GT, D])
        value = sb("value", [P, GT, D])
        attn = sb("attn", [P, 2, 2, 3 * P])
        retrieved = sb("retrieved", [P, HALF])
        act = sb("act", [P, 2, GT * P])
        act_hi = sb("act_hi", [P, 2, GT * P], fp32r)
        act_lo = sb("act_lo", [P, 2, GT * P], fp32r)
        logits_ch = sb("logits_ch", [P, HALF])
        top = sb("top", [P, GT])
        below = sb("below", [P, GT, EXPERTS])
        ranked = sb("ranked", [P, GT, EXPERTS])
        first = sb("first", [P, GT])
        chosen = sb("chosen", [P, GT, EXPERTS])
        exps = sb("exps", [P, GT, EXPERTS])
        total = sb("total", [P, GT])
        top_prob = sb("top_prob", [P, GT])
        weight = sb("weight", [P, 2 * GT, EXPERTS])
        weight_ch = sb("weight_ch", [GT * EXPERTS, P])
        picked = sb("picked", [P, GT, EXPERTS * D])
        down_raw = picked[:, 0:2, :]
        add4 = sb("add4", [P, 2, 4 * D])
        add2 = sb("add2", [P, 2, 2 * D])
        expert_out = sb("expert_out", [P, GT, D])
        base = sb("base", [P, GT, D])
        result = sb("result", [P, GT, D])
        carrier = sb("carrier", [P, 1])
        carried = sb("carried", [P, 1])
        warm = sb("warm", [P, 1])

        bank = [ctx.enter_context(nc.psum_tensor(f"bank{b}", [P, 512], fp32)) for b in range(8)]
        full = [sem(f"bank{b}_full") for b in range(8)]
        free = [sem(f"bank{b}_free") for b in range(8)]

        s_x = sem("s_x")
        s_conv_w = sem("s_conv_w")
        s_edge_rows = sem("s_edge_rows")
        s_loads = sem("s_loads")
        s_const = sem("s_const")
        s_row_const = sem("s_row_const")
        s_ident = sem("s_ident")
        s_zero = sem("s_zero")
        s_norm = sem("s_norm")
        s_sqrt = sem("s_sqrt")
        s_setup_pe = sem("s_setup_pe")
        s_x_float = sem("s_x_float")
        s_edge_cols = sem("s_edge_cols")
        s_edge_diff = sem("s_edge_diff")
        s_conv_ready = sem("s_conv_ready")
        s_weights_ready = sem("s_weights_ready")
        gathered = [sem(f"gathered{h}") for h in range(2)]
        gather_ready = sem("gather_ready")
        window_cols = sem("window_cols")
        rstd_ready = {s: sem(f"rstd_ready{s}") for s in (1, 2)}
        normed_ready = {s: sem(f"normed_ready{s}") for s in (1, 2)}
        folded_ready = sem("folded_ready")
        feature_ready = sem("feature_ready")
        split_hi = sem("split_hi")
        value_part = sem("value_part")
        wait_carried = sem("wait_carried")
        split_ready = sem("split_ready")
        expert_sum = sem("expert_sum")
        exps_ready = sem("exps_ready")
        weight_ready = sem("weight_ready")
        result_ready = sem("result_ready")
        stored = sem("stored")
        chain_ln = {s: sem(f"chain_ln{s}") for s in (1, 2)}
        chain_soft = sem("chain_soft")
        chain_adds = sem("chain_adds")
        chain_setup = sem("chain_setup")

        LN_STEPS, SOFT_STEPS, ADD_STEPS, SETUP_STEPS = 8, 6, 8, 10
        ZEROED, CONSTS_EARLY, CONSTS, LOADS = 6, 7, 9, 38

        block = ctx.enter_context(nc.Block())

        def emit(body):
            def program(eng):
                lead = LAG_FFN + 1
                for i in range(lead):
                    body(eng, i)
                if groups - 1 > lead:
                    with eng.Fori(lead, groups - 1) as i:
                        body(eng, i)
                for i in range(max(groups - 1, lead), iterations):
                    body(eng, i)
            return program

        def runs(i, lag):
            return not isinstance(i, int) or 0 <= i - lag < groups

        def windows_first(i):
            return isinstance(i, int) and i < LAG_FFN

        def wait_full(eng, job, i):
            eng.wait_ge(full[BANK_OF[job]], jobs_before(job, i, groups) + 1)

        def wait_free(eng, job, i):
            n = jobs_before(job, i, groups)
            if not isinstance(n, int) or n > 0:
                eng.wait_ge(free[BANK_OF[job]], n)

        def wait_taken(eng, job, i):
            eng.wait_ge(free[BANK_OF[job]], jobs_before(job, i, groups) + 1)

        def tiles_of(ap, g):
            return ap[:, bass.ds(g * GT, GT), :]

        def by_half(b):
            return bank[b][:, :].rearrange("p (s h d) -> p h s d", h=2, d=D)

        @block.sync
        def _(sp):
            n_rows = tiles
            sp.dma_start(x_rows[0:n_rows, :], x.rearrange("(t p) -> t p", p=P)[0:n_rows, :]).then_inc(s_x, 16)
            k = EDGE + KSIZE
            sp.dma_start(edge_rows[0:EDGE, :], emb[0:1, :].broadcast_to([EDGE, D])).then_inc(s_edge_rows, 16)
            sp.dma_start(edge_rows[EDGE:k, :], emb[0:KSIZE, :]).then_inc(s_edge_rows, 16)
            sp.dma_start(edge_rows[k:k + KSIZE, :], emb[LAST_START:VOCAB, :]).then_inc(s_edge_rows, 16)
            sp.dma_start(edge_rows[k + KSIZE:2 * k, :],
                         emb[VOCAB - 1:VOCAB, :].broadcast_to([EDGE, D])).then_inc(s_edge_rows, 16)
            whole = (BLOCKS - 1) * P
            sp.dma_start(conv_wt[:, 0:BLOCKS - 1, :],
                         conv_w[0:whole, :].rearrange("(k p) o -> p k o", p=P)).then_inc(s_conv_w, 16)
            sp.dma_start(conv_wt[0:D, BLOCKS - 1, :], conv_w[whole:WINDOW, :]).then_inc(s_conv_w, 16)
            sp.dma_start(conv_wt[TAIL - 1:TAIL, BLOCKS - 1, :],
                         conv_b.rearrange("(a o) -> a o", a=1)).then_inc(s_conv_w, 16)
            sp.dma_start(conv_rows[:, :, :], conv_w.rearrange("(k p) o -> p k o", p=D)).then_inc(s_conv_w, 16)

            sp.wait_ge(s_zero, ZEROED)
            loads = []
            for r in (0, D):
                loads += [(kq_raw[r:r + D, 0:D], kw1), (kq_raw[r:r + D, D:P], qw1), (v_raw[r:r + D, 0:D], vw), (up_raw[r:r + D, :], w1)]
            for c in (0, PHASES):
                loads += [(phase_k_w[0:D, c:c + PHASES], kw2), (phase_q_w[D:P, c:c + PHASES], qw2)]
            loads += [(gate_w[:, :, 0:EXPERTS], wg.rearrange("(k p) e -> p k e", p=P))]
            wd_v = wd.rearrange("e (k p) d -> k p e d", p=P)
            for c in range(2):
                loads += [(down_raw[:, c, :].rearrange("p (e d) -> p e d", e=EXPERTS), wd_v[c])]
            for t in range(GT):
                loads += [(down_b[t * EXPERTS:(t + 1) * EXPERTS, t * D:(t + 1) * D], bd)]

            def column(v):
                return v.rearrange("(p a) -> p a", a=1)

            loads += [(hidden_b[0:D, :], column(kb1)), (hidden_b[D:P, :], column(qb1)),
                      (v_b[:, :], vb.rearrange("(a d) -> a d", a=1).broadcast_to([P, D])),
                      (gate_b[0:EXPERTS, :], column(bg)), (gate_b[D:D + EXPERTS, :], column(bg)),
                      (up_b[:, 0:1], column(b1[0:P])), (up_b[:, 1:2], column(b1[P:HIDDEN]))]
            for r in range(0, P, PHASES):
                loads += [(phase_k_b[r:r + PHASES, :], column(kb2)), (phase_q_b[r:r + PHASES, :], column(qb2))]
            assert len(loads) == LOADS
            for dst, src in loads:
                sp.dma_start(dst, src).then_inc(s_loads, 16)

            def store(eng, i):
                if runs(i, LAG_FFN):
                    g = i - LAG_FFN
                    eng.wait_ge(result_ready, g + 1)
                    dst = out.rearrange("(t p) d -> p t d", p=P)[:, bass.ds(g * GT, GT), :]
                    eng.dma_start(dst, result[:, :, :]).then_inc(stored, 16)

            emit(store)(sp)
            sp.wait_ge(stored, 16 * groups)

        @block.gpsimd
        def _(pool):
            G = nc.gpsimd
            G.memset(ident[:, :], 0.0).then_inc(s_ident, 1)
            pool.wait_ge(s_ident, 1)
            G.affine_select(out=ident[:, :], in_=ident[:, :], compare_op=ALU.not_equal, fill=1.0, base=0,
                            pattern=[[-1, P]], channel_multiplier=1).then_inc(s_ident, 1)
            for tile in (v_raw, phase_k_w, phase_q_w, gate_w, gate_b, down_b):
                ap = tile[:, :, :] if len(tile.shape) == 3 else tile[:, :]
                G.memset(ap, 0.0).then_inc(s_zero, 1)
            G.iota(edge_ids[:, 0:EDGE], pattern=[[1, EDGE]], base=-REACH, channel_multiplier=0,
                   allow_small_or_imprecise_dtypes=True).then_inc(s_const, 1)
            G.iota(edge_ids[:, EDGE:2 * EDGE], pattern=[[1, EDGE]], base=VOCAB - REACH, channel_multiplier=0,
                   allow_small_or_imprecise_dtypes=True).then_inc(s_const, 1)
            G.iota(priority[:, :], pattern=[[-1, EXPERTS]], base=EXPERTS, channel_multiplier=0,
                   allow_small_or_imprecise_dtypes=True).then_inc(s_const, 1)
            G.memset(window[:, :, WIN_COLS - 1:WIN_COLS], 1.0).then_inc(s_const, 1)
            G.memset(minus_half[:, :], -0.5).then_inc(s_const, 1)
            G.memset(weight[:, :, :], 0.0).then_inc(s_const, 1)
            G.memset(feature_q[:, :, :], 0.0).then_inc(s_const, 1)
            G.iota(norm[:, :], pattern=[[PHASES, 3 * P]], base=PHASES, channel_multiplier=0,
                   allow_small_or_imprecise_dtypes=True).then_inc(s_norm, 1)
            pool.wait_ge(s_norm, 1)
            G.iota(norm[:, 2 * P:3 * P], pattern=[[PHASES, P]], base=PHASES * (P + 1), channel_multiplier=0,
                   allow_small_or_imprecise_dtypes=True).then_inc(s_norm, 1)
            def gather(eng, g, half, i=None):
                if i is not None:
                    wait_full(eng, f"window{BLOCKS * half + BLOCKS - 1}", i)
                    eng.wait_ge(gather_ready, g + 1)
                    if not isinstance(g, int) or g > 1 or half > 0:
                        eng.wait_ge(wait_carried, 2 * (g - 1) + half)
                    G.tensor_tensor(carrier[:, :], minus_half[:, 0:1], minus_half[:, 0:1], ALU.add)\
                        .then_inc(wait_carried, 1)
                for t in range(4 * half, 4 * half + 4):
                    eng.indirect_dma_start(
                        out=window[:, t, 0:WINDOW], out_offset=None, in_=emb,
                        in_offset=bass.IndirectOffsetOnAxis(ap=start8[:, t:t + 1], axis=0),
                    ).then_inc(gathered[half], 16)

            pool.wait_ge(gather_ready, 1)
            gather(pool, 0, 0)
            gather(pool, 0, 1)
            pool.wait_ge(s_norm, 3)
            G.affine_select(out=mask[:, 0:2 * P], in_=mask[:, 0:2 * P], compare_op=ALU.is_ge, fill=0.0, base=0,
                            pattern=[[1, 2 * P]], channel_multiplier=-1).then_inc(s_const, 1)
            G.affine_select(out=mask[:, 2 * P:3 * P], in_=mask[:, 2 * P:3 * P], compare_op=ALU.is_ge, fill=0.0,
                            base=0, pattern=[[1, P]], channel_multiplier=-1).then_inc(s_const, 1)

            def inverse_root(eng, s, g):
                eng.wait_ge(chain_ln[s], g * LN_STEPS + 6)
                G.tensor_tensor(rstd[s][:, :], variance[s][:, :], minus_half[:, :], ALU.pow)\
                    .then_inc(rstd_ready[s], 1)

            def body(eng, i):
                attend, ffn, more = runs(i, LAG_ATTEND), runs(i, LAG_FFN), runs(i + 1, LAG_CONV)
                g = i - LAG_FFN
                chain = Chain(eng, chain_adds, g, ADD_STEPS)

                def add_pair(pair, before_last=None):
                    two = slice(2 * pair, 2 * pair + 2)
                    wait_taken(eng, f"expert{2 * pair + 1}", i)
                    chain(G.tensor_tensor(add4[:, :, :], picked[:, two, 0:4 * D], picked[:, two, 4 * D:8 * D],
                                          ALU.add))
                    chain(G.tensor_tensor(add2[:, :, :], add4[:, :, 0:2 * D], add4[:, :, 2 * D:4 * D], ALU.add))
                    last = G.tensor_tensor(expert_out[:, two, :], add2[:, :, 0:D], add2[:, :, D:2 * D], ALU.add)
                    if pair == GT // 2 - 1:
                        last.then_inc(expert_sum, 1)

                if more:
                    gather(eng, i + 1, 0, i)
                if attend:
                    inverse_root(eng, 2, i - LAG_ATTEND)
                if more:
                    gather(eng, i + 1, 1, i)
                if ffn:
                    add_pair(0)
                    add_pair(1)
                if runs(i, LAG_CONV):
                    inverse_root(eng, 1, i)
                if ffn:
                    add_pair(2)
                    add_pair(3)
                    chain.end()
                    eng.wait_ge(expert_sum, g + 1)
                    wait_taken(eng, "down_bias", i)
                    if not isinstance(g, int) or g > 0:
                        eng.wait_ge(stored, 16 * g)
                    G.tensor_tensor(result[:, :, :], expert_out[:, :, :], base[:, :, :], ALU.add)\
                        .then_inc(result_ready, 1)

            emit(body)(pool)

        @block.scalar
        def _(sc):
            S = nc.scalar
            sc.wait_ge(s_norm, 2)
            S.activation(norm[:, :], norm[:, :], ACT.Sqrt).then_inc(s_sqrt, 1)
            sc.wait_ge(s_edge_cols, 1)
            S.activation(edge_cols[:, :], bank[7][0:D, 0:2 * (EDGE + KSIZE)], ACT.Copy).then_inc(s_edge_cols, 1)
            sc.wait_ge(s_row_const, 12)

            def copy_out(eng, dst, job, i):
                wait_full(eng, job, i)
                S.activation(dst, bank[BANK_OF[job]][:, :], ACT.Copy).then_inc(free[BANK_OF[job]], 1)

            def copy_window(eng, n, i):
                half, k = divmod(n, BLOCKS)
                rows = P if k < BLOCKS - 1 else TAIL
                job = f"window{n}"
                wait_full(eng, job, i)
                S.activation(window_t[0:rows, k, half * HALF:(half + 1) * HALF], bank[BANK_OF[job]][0:rows, :],
                             ACT.Copy).then_inc(free[BANK_OF[job]], 1)

            def body(eng, i):
                conv, features, attend, ffn = (runs(i, lag) for lag in
                                               (LAG_CONV, LAG_FEATURES, LAG_ATTEND, LAG_FFN))

                def halves(ap, half):
                    return ap[:, half * HALF:(half + 1) * HALF]

                def windows(*which):
                    for n in which:
                        if conv:
                            copy_window(eng, n, i)

                def later_windows(*which):
                    if not windows_first(i):
                        windows(*which)

                if isinstance(i, int) and i == LAG_FEATURES:
                    eng.wait_ge(s_loads, 16 * LOADS)
                if windows_first(i):
                    windows(*range(2 * BLOCKS))
                if ffn:
                    g = i - LAG_FFN
                    for half in range(2):
                        copy_out(eng, halves(normed_t[2], half), f"ffn_in{half}", i)
                if ffn:
                    for n in range(4):
                        half, part = divmod(n, 2)
                        job = f"up{n}"
                        if n == 2:
                            later_windows(0, 1)
                        wait_full(eng, job, i)
                        S.activation(act[:, part, half * HALF:(half + 1) * HALF], bank[BANK_OF[job]][:, :],
                                     ACT.Gelu, bias=up_b[:, part:part + 1]).then_inc(free[BANK_OF[job]], 1)
                else:
                    later_windows(0, 1)
                later_windows(2)
                if features:
                    for half in range(2):
                        copy_out(eng, halves(normed_t[1], half), f"attn_in{half}", i)
                if attend:
                    copy_out(eng, retrieved[:, :], "retrieved", i)
                if features:
                    for half in range(2):
                        job = f"hidden{half}"
                        wait_full(eng, job, i)
                        S.activation(halves(hidden, half), bank[BANK_OF[job]][:, :],
                                     ACT.Tanh, bias=hidden_b[:, 0:1]).then_inc(free[BANK_OF[job]], 1)
                later_windows(3)
                if ffn:
                    S.activation(warm[:, :], sin_shift[:, :], ACT.Exp)
                    wait_full(eng, "gate", i)
                    S.activation(logits_ch[:, :], bank[4][:, :], ACT.Identity, bias=gate_b[:, 0:1])\
                        .then_inc(free[4], 1)
                later_windows(4, 5)
                if ffn:
                    eng.wait_ge(chain_soft, g * SOFT_STEPS + 2)
                    S.activation(exps[:, :, :], below[:, :, :], ACT.Exp).then_inc(exps_ready, 1)
                later_windows(6, 7, 8, 9)
                if ffn:
                    wait_full(eng, "weights_ch", i)
                    S.activation(weight_ch[:, :], bank[3][0:GT * EXPERTS, 0:P], ACT.Copy).then_inc(free[3], 1)
                if features:
                    for s, bias in (("k", phase_k_b), ("q", phase_q_b)):
                        job = f"phase_{s}"
                        wait_full(eng, job, i)
                        S.activation(turn[s][:, :], bank[BANK_OF[job]][:, :], ACT.Tanh, bias=bias[:, 0:1])\
                            .then_inc(free[BANK_OF[job]], 1)

                    def sine(dst, s, rows):
                        S.activation(dst, folded[s][rows, :], ACT.Sin, scale=sin_scale[rows, 0:1],
                                     bias=sin_shift[rows, 0:1]).then_inc(feature_ready, 1)

                    g = i - LAG_FEATURES
                    eng.wait_ge(folded_ready, 2 * g + 1)
                    sine(feature_k[:, :], "k", slice(0, P))
                    eng.wait_ge(folded_ready, 2 * g + 2)
                    for half in range(2):
                        rows = slice(half * D, (half + 1) * D)
                        sine(feature_q[rows, half, :], "q", rows)
                S.activation(warm[:, :], sin_shift[:, :], ACT.Gelu)
                if conv:
                    copy_out(eng, conv_ch[:, :], "conv", i)
                    wait_full(eng, "conv_tok", i)
                    S.activation(tiles_of(h_all, i).rearrange("p (h s) d -> p h s d", h=2), by_half(3),
                                 ACT.Copy).then_inc(free[3], 1)

            emit(body)(sc)

        @block.vector
        def _(dve):
            V = nc.vector
            link = Chain(dve, chain_setup, 0, SETUP_STEPS)
            for q in range(4):
                rows = slice(32 * q, 32 * q + 32)
                cosine = q % 2 == 0
                V.memset(fold[rows, :], -1.0 if cosine else 1.0).then_inc(s_row_const, 1)
                V.memset(sin_scale[rows, :], -PI_BELOW if cosine else PI_BELOW).then_inc(s_row_const, 1)
                V.memset(sin_shift[rows, :], float(np.pi / 2) if cosine else 0.0).then_inc(s_row_const, 1)
            dve.wait_ge(s_x, 16)
            V.tensor_copy(x_float[0:tiles, :], x_rows[0:tiles, :]).then_inc(s_x_float, 1)
            dve.wait_ge(s_x_float, 1)
            link(V.tensor_scalar(x_float[0:tiles, :], x_float[0:tiles, :], float(-REACH),
                                 float(VOCAB + REACH - 1), ALU.max, ALU.min))
            dve.wait_ge(s_setup_pe, 1)
            link(V.tensor_copy(x_edge[:, 0:tiles], bank[6][:, 0:tiles]))
            link(V.tensor_scalar(x_start_f[:, 0:tiles], x_edge[:, 0:tiles], float(-REACH), 0.0, ALU.add, ALU.max))
            link(V.tensor_scalar(x_start_f[:, 0:tiles], x_start_f[:, 0:tiles], float(LAST_START), None, ALU.min))
            link(V.tensor_copy(x_start[:, 0:tiles], x_start_f[:, 0:tiles]))

            def prepare_starts(g):
                V.tensor_copy(start8[:, :], x_start[:, bass.ds(g * GT, GT)]).then_inc(gather_ready, 1)

            def prepare_edges(g):
                V.tensor_tensor(window[:, :, WINDOW:WINDOW + 2 * EDGE],
                                over_last(x_edge[:, bass.ds(g * GT, GT)], 2 * EDGE),
                                edge_ids[:, :].unsqueeze(1).broadcast_to([P, GT, 2 * EDGE]),
                                ALU.is_equal).then_inc(window_cols, 1)

            prepare_starts(0)
            dve.wait_ge(s_const, CONSTS_EARLY)
            prepare_edges(0)
            dve.wait_ge(s_sqrt, 1)
            V.reciprocal(mask[:, :], norm[:, :]).then_inc(s_norm, 1)
            dve.wait_ge(s_edge_cols, 2)
            k = EDGE + KSIZE
            for j in range(KSIZE):
                V.tensor_tensor(edge_diff[:, j, 0:EDGE], edge_cols[:, j:j + EDGE],
                                edge_cols[:, EDGE + j:EDGE + j + 1].broadcast_to([D, EDGE]),
                                ALU.subtract).then_inc(s_edge_diff, 1)
                V.tensor_tensor(edge_diff[:, j, EDGE:2 * EDGE], edge_cols[:, k + 1 + j:k + 1 + j + EDGE],
                                edge_cols[:, k + j:k + j + 1].broadcast_to([D, EDGE]),
                                ALU.subtract).then_inc(s_edge_diff, 1)
            dve.wait_ge(s_setup_pe, 3)
            V.tensor_copy(conv_wt[D:D + 2 * EDGE, BLOCKS - 1, :], bank[6][D:D + 2 * EDGE, 0:D])\
                .then_inc(s_conv_ready, 1)
            dve.wait_ge(s_const, CONSTS)
            dve.wait_ge(s_row_const, 12)

            def split_feature_weights():
                dve.wait_ge(s_loads, 16 * LOADS)
                link(V.tensor_copy(kq_hi[:, :], kq_raw[:, :]))
                V.tensor_tensor(kq_lo[:, :], kq_raw[:, :], kq_hi[:, :].bitcast(fp32), ALU.subtract)\
                    .then_inc(s_weights_ready, 1)
                link(V.tensor_copy(v_parts[:, 0:D], v_raw[:, 0:D]))
                V.tensor_copy(v_parts[:, 2 * D:4 * D], v_raw[:, D:3 * D]).then_inc(s_weights_ready, 1)
                V.tensor_tensor(v_parts[:, D:2 * D], v_raw[:, 0:D], v_parts[:, 0:D].bitcast(fp32), ALU.subtract)\
                    .then_inc(s_weights_ready, 1)

            def split_ffn_weights():
                link(V.tensor_copy(up_hi[:, :], up_raw[:, :]))
                V.tensor_tensor(up_lo[:, :], up_raw[:, :], up_hi[:, :].bitcast(fp32), ALU.subtract)\
                    .then_inc(s_weights_ready, 1)
                for c in range(2):
                    link(V.tensor_copy(down_hi[:, c, :], down_raw[:, c, :]))
                    V.tensor_tensor(down_lo[:, c, :], down_raw[:, c, :], down_hi[:, c, :].bitcast(fp32),
                                    ALU.subtract).then_inc(s_weights_ready, 1)
                link.end()

            def norm_centre(eng, s, g):
                chain = Chain(eng, chain_ln[s], g, LN_STEPS)
                h = tiles_of(h_all, g)
                chain(V.tensor_reduce(sums[s][:, :], h, axis=AX, op=ALU.add))
                chain(V.tensor_scalar(neg_mean[s][:, :], sums[s][:, :], -1.0 / D, None, ALU.mult))
                chain(V.tensor_tensor(centred[s][:, :, :], h, over_last(neg_mean[s][:, :], D), ALU.add))
                return chain

            def norm_variance(s, chain):
                chain(V.tensor_tensor(squares[:, :, :], centred[s][:, :, :], centred[s][:, :, :], ALU.mult))
                chain(V.tensor_reduce(sums[s][:, :], squares[:, :, :], axis=AX, op=ALU.add))
                chain(V.tensor_scalar(variance[s][:, :], sums[s][:, :], 1.0 / D, EPS, ALU.mult, ALU.add))

            def norm_apply(eng, s, g):
                chain = Chain(eng, chain_ln[s], g, LN_STEPS, done=6)
                eng.wait_ge(rstd_ready[s], g + 1)
                chain(V.tensor_tensor(squares[:, :, :], centred[s][:, :, :], over_last(rstd[s][:, :], D), ALU.mult))
                hi, lo = normed[s][:, :, 0, :], normed[s][:, :, 1, :]
                chain(V.tensor_copy(hi.bitcast(fp32r), squares[:, :, :]))
                V.tensor_tensor(lo, squares[:, :, :], hi, ALU.subtract).then_inc(normed_ready[s], 1)
                chain.end()

            def expert(eng, t, i):
                job = f"expert{t}"
                g = i - LAG_FFN
                if t == 0:
                    eng.wait_ge(weight_ready, g + 1)
                    if not isinstance(g, int) or g > 0:
                        eng.wait_ge(expert_sum, g)
                wait_full(eng, job, i)
                V.tensor_tensor(picked[:, t, :].rearrange("p (e d) -> p e d", e=EXPERTS),
                                bank[BANK_OF[job]][:, :].rearrange("p (e d) -> p e d", e=EXPERTS),
                                over_last(weight[:, t, :], D), ALU.mult).then_inc(free[BANK_OF[job]], 1)

            def body(eng, i):
                conv, features, attend, ffn = (runs(i, lag) for lag in
                                               (LAG_CONV, LAG_FEATURES, LAG_ATTEND, LAG_FFN))

                def picks(*which):
                    for t in which:
                        if ffn:
                            expert(eng, t, i)

                def mask_scores(seq, part):
                    cols, at = (SEQ, 0) if part == "early" else (P, SEQ)
                    job = f"scores{seq}_{part}"
                    b = BANK_OF[job]
                    wait_full(eng, job, i)
                    V.tensor_tensor(attn[:, seq, :, at:at + cols],
                                    bank[b][:, 0:2 * cols].rearrange("p (h c) -> p h c", h=2),
                                    mask[:, at:at + cols].unsqueeze(1).broadcast_to([P, 2, cols]),
                                    ALU.mult).then_inc(free[b], 1)

                def values():
                    if features:
                        for n in range(2):
                            job = f"value{n}"
                            wait_full(eng, job, i)
                            parts = bank[BANK_OF[job]][:, :].rearrange("p (t a d) -> p t a d", t=4, a=2)
                            four = slice(4 * n, 4 * n + 4)
                            V.tensor_tensor(value_hi[:, four, :], parts[:, :, 0, :],
                                            v_b[:, :].unsqueeze(1).broadcast_to([P, 4, D]), ALU.add)\
                                .then_inc(value_part, 1)
                            eng.wait_ge(value_part, 2 * (i - LAG_FEATURES) + n + 1)
                            V.tensor_tensor(value[:, four, :], value_hi[:, four, :], parts[:, :, 1, :], ALU.add)\
                                .then_inc(free[BANK_OF[job]], 1)

                def act_part(ap, n):
                    half, part = divmod(n, 2)
                    return ap[:, part, half * HALF:(half + 1) * HALF]

                def split_high(*which):
                    for n in which:
                        if ffn:
                            wait_taken(eng, f"up{n}", i)
                            V.tensor_copy(act_part(act_hi, n), act_part(act, n)).then_inc(split_hi, 1)

                def split_low(*which):
                    for n in which:
                        if ffn:
                            eng.wait_ge(split_hi, (i - LAG_FFN) * 4 + n + 1)
                            V.tensor_tensor(act_part(act_lo, n), act_part(act, n), act_part(act_hi, n).bitcast(fp32),
                                            ALU.subtract).then_inc(split_ready, 1)

                if attend:
                    mask_scores(0, "early")
                if runs(i + 1, LAG_CONV):
                    eng.wait_ge(gathered[1], 64 * (i + 1))
                    prepare_starts(i + 1)
                if isinstance(i, int) and i == LAG_FEATURES:
                    split_feature_weights()
                if features:
                    norm_apply(eng, 1, i - LAG_FEATURES)
                if isinstance(i, int) and i == LAG_FEATURES:
                    split_ffn_weights()
                if attend:
                    mask_scores(0, "late")
                    mask_scores(1, "early")
                    mask_scores(1, "late")
                split_high(0, 1)
                split_low(0)
                split_high(2)
                split_low(1)
                split_high(3)
                split_low(2)
                if not ffn:
                    values()
                if attend:
                    wait_full(eng, "retrieved_tok", i)
                    h = tiles_of(h_all, i - LAG_ATTEND).rearrange("p (h s) d -> p h s d", h=2)
                    V.tensor_tensor(h, h, by_half(3), ALU.add).then_inc(free[3], 1)
                    wait_taken(eng, "retrieved_tok", i)
                split_low(3)
                if attend:
                    ln = norm_centre(eng, 2, i - LAG_ATTEND)
                if ffn:
                    g = i - LAG_FFN
                    wait_full(eng, "gate_tok", i)
                    chain = Chain(eng, chain_soft, g, SOFT_STEPS)
                    logits = by_half(5)[:, :, :, 0:EXPERTS]
                    chain(V.tensor_reduce(top[:, :].rearrange("p (h s) -> p h s", h=2), logits, axis=AX, op=ALU.max))
                    chain(V.tensor_tensor(
                        below[:, :, :].rearrange("p (h s) e -> p h s e", h=2), logits,
                        top[:, :].rearrange("p (h s) -> p h s", h=2).unsqueeze(3)
                        .broadcast_to([P, 2, 4, EXPERTS]), ALU.subtract))
                    V.scalar_tensor_tensor(ranked[:, :, :], below[:, :, :], 0.0,
                                           priority[:, :].unsqueeze(1).broadcast_to([P, GT, EXPERTS]),
                                           ALU.is_equal, ALU.mult).then_inc(free[5], 1)
                if ffn:
                    wait_taken(eng, "gate_tok", i)
                    chain(V.tensor_reduce(first[:, :], ranked[:, :, :], axis=AX, op=ALU.max))
                    chain(V.tensor_tensor(chosen[:, :, :], ranked[:, :, :], over_last(first[:, :], EXPERTS),
                                          ALU.is_equal))
                if ffn:
                    values()
                if ffn:
                    eng.wait_ge(exps_ready, g + 1)
                    chain(V.tensor_reduce(total[:, :], exps[:, :, :], axis=AX, op=ALU.add))
                    chain(V.reciprocal(top_prob[:, :], total[:, :]))
                    V.tensor_tensor(weight[:, 0:GT, :], chosen[:, :, :], over_last(top_prob[:, :], EXPERTS),
                                    ALU.mult).then_inc(weight_ready, 1)
                    chain.end()
                picks(0)
                if attend:
                    norm_variance(2, ln)
                picks(1, 2)
                if runs(i + 1, LAG_CONV):
                    wait_full(eng, "window9", i)
                    prepare_edges(i + 1)
                if features:
                    for s in "kq":
                        wait_taken(eng, f"phase_{s}", i)
                        V.scalar_tensor_tensor(folded[s][:, :], turn[s][:, :], fold[:, 0:1], turn[s][:, :],
                                               ALU.mult, ALU.max).then_inc(folded_ready, 1)
                if ffn:
                    wait_full(eng, "down_bias", i)
                    if not isinstance(g, int) or g > 0:
                        eng.wait_ge(result_ready, g)
                    V.tensor_tensor(base[:, :, :], tiles_of(h_all, g),
                                    bank[2][:, :].rearrange("p (t d) -> p t d", t=GT), ALU.add)\
                        .then_inc(free[2], 1)
                picks(3, 4)
                if attend:
                    norm_apply(eng, 2, i - LAG_ATTEND)
                picks(5)
                if conv:
                    wait_taken(eng, "conv_tok", i)
                    V.tensor_copy(carried[:, :], minus_half[:, 0:1])
                    ln = norm_centre(eng, 1, i)
                picks(6)
                if conv:
                    norm_variance(1, ln)
                picks(7)

            emit(body)(dve)

        @block.tensor
        def _(pe):
            T = nc.tensor
            pe.wait_ge(s_ident, 2)
            pe.wait_ge(chain_setup, 1)
            T.transpose(bank[6][:, 0:tiles], x_float[0:tiles, :], ident[0:tiles, 0:tiles]).then_inc(s_setup_pe, 1)
            k = 2 * (EDGE + KSIZE)
            pe.wait_ge(s_edge_rows, 64)
            T.transpose(bank[7][0:D, 0:k], edge_rows[:, :], ident[0:k, 0:k]).then_inc(s_edge_cols, 1)
            pe.wait_ge(s_conv_w, 64)
            pe.wait_ge(s_edge_diff, 2 * KSIZE)
            pe.wait_ge(chain_setup, 2)
            for j in range(KSIZE):
                last = T.matmul(bank[6][D:D + 2 * EDGE, 0:D], edge_diff[:, j, :], conv_rows[:, j, :],
                                start=(j == 0), stop=(j == KSIZE - 1))
            last.then_inc(s_setup_pe, 2)

            def token_to_channel(src, job, i):
                half = int(job[-1])
                wait_free(pe, job, i)
                for s in range(4):
                    last = T.transpose(bank[BANK_OF[job]][:, s * P:(s + 1) * P],
                                       src[:, 4 * half + s, :, :].rearrange("p a d -> p (a d)"), ident[:, :])
                last.then_inc(full[BANK_OF[job]], 1)

            def channel_to_token(src, job, i):
                wait_free(pe, job, i)
                for s in range(4):
                    last = T.transpose(bank[BANK_OF[job]][:, s * P:(s + 1) * P], src[:, s * P:(s + 1) * P],
                                       ident[:, :])
                last.then_inc(full[BANK_OF[job]], 1)

            def window_transpose(n, i):
                half, k = divmod(n, BLOCKS)
                if k == 0:
                    pe.wait_ge(gathered[half], 64 * (i + 1))
                if n == 4:
                    pe.wait_ge(window_cols, i + 1)
                job = f"window{n}"
                cols = slice(k * P, min((k + 1) * P, WIN_COLS))
                rows = cols.stop - cols.start
                wait_free(pe, job, i)
                for s in range(4):
                    last = T.transpose(bank[BANK_OF[job]][0:rows, s * P:(s + 1) * P],
                                       window[:, 4 * half + s, cols], ident[:, :])
                last.then_inc(full[BANK_OF[job]], 1)

            def by_halves(job, weights, src, i, k_rows=(P,)):
                b = BANK_OF[job]
                wait_free(pe, job, i)
                for k, rows in enumerate(k_rows):
                    for half in range(2):
                        last = T.matmul(bank[b][half * D:(half + 1) * D, :], weights(k)[0:rows, :],
                                        src(k)[0:rows, half * HALF:(half + 1) * HALF],
                                        start=(k == 0), stop=(k == len(k_rows) - 1))
                last.then_inc(full[b], 1)

            def two_parts(out_ap, hi, lo, src):
                T.matmul(out_ap, hi, src, start=True, stop=False)
                return T.matmul(out_ap, lo, src, start=False, stop=True)

            def expert(t, i):
                job = f"expert{t}"
                b = BANK_OF[job]
                pe.wait_ge(split_ready, (i - LAG_FFN) * 4 + (2 if t < 4 else 4))
                wait_free(pe, job, i)
                cols = slice(t * P, (t + 1) * P)
                products = [(act_hi, down_hi), (act_hi, down_lo), (act_lo, down_hi)]
                for k in range(2):
                    for n, (a, w) in enumerate(products):
                        last = T.matmul(bank[b][:, :], a[:, k, cols], w[:, k, :],
                                        start=(k == 0 and n == 0), stop=(k == 1 and n == 2))
                last.then_inc(full[b], 1)

            def body(eng, i):
                conv, features, attend, ffn = (runs(i, lag) for lag in
                                               (LAG_CONV, LAG_FEATURES, LAG_ATTEND, LAG_FFN))

                def windows(*which):
                    for n in which:
                        if conv:
                            window_transpose(n, i)

                def later_windows(*which):
                    if not windows_first(i):
                        windows(*which)

                def experts(*which):
                    for t in which:
                        if ffn:
                            expert(t, i)

                def scores(seq, part):
                    job = f"scores{seq}_{part}"
                    b = BANK_OF[job]
                    first = seq * SEQ + (P if part == "late" else 0)
                    n = (seq + 1) * SEQ - first
                    wait_free(eng, job, i)
                    T.matmul(bank[b][:, 0:2 * n].rearrange("p (h c) -> p h c", h=2),
                             feature_k[:, first:first + P], feature_q[:, :, first:first + n],
                             start=True, stop=True).then_inc(full[b], 1)

                def retrieve():
                    wait_free(eng, "retrieved", i)
                    for seq in range(2):
                        wait_taken(eng, f"scores{seq}_late", i)
                        for part in range(2):
                            for half in range(2):
                                last = T.matmul(
                                    bank[2][half * D:(half + 1) * D, seq * SEQ + part * P:(seq + 1) * SEQ],
                                    value[:, 4 * half + 2 * seq + part, :],
                                    attn[:, seq, half, (0 if part == 0 else SEQ):SEQ + part * P],
                                    start=(part == 0), stop=(part == 1), skip_group_check=True)
                    last.then_inc(full[2], 1)

                def up(*which):
                    for n in which:
                        if ffn:
                            half, part = divmod(n, 2)
                            job = f"up{n}"
                            wait_taken(eng, f"ffn_in{half}", i)
                            wait_free(eng, job, i)
                            cols = slice(part * P, (part + 1) * P)
                            two_parts(bank[BANK_OF[job]][:, :], up_hi[:, cols], up_lo[:, cols],
                                      normed_t[2][:, half * HALF:(half + 1) * HALF])\
                                .then_inc(full[BANK_OF[job]], 1)

                def values(half):
                    if features:
                        job = f"value{half}"
                        b = BANK_OF[job]
                        wait_free(eng, job, i)
                        for s in range(4):
                            cols = slice((4 * half + s) * P, (4 * half + s + 1) * P)
                            n = 2 * P if s < 3 else P
                            last = T.matmul(bank[b][:, s * P:s * P + n], normed_t[1][:, cols], v_parts[:, 0:n],
                                            start=True, stop=True)
                        last.then_inc(full[b], 1)

                if windows_first(i):
                    windows(*range(2 * BLOCKS))
                if ffn:
                    if isinstance(i, int) and i == LAG_FFN:
                        eng.wait_ge(s_weights_ready, 6)
                    eng.wait_ge(normed_ready[2], i - LAG_FFN + 1)
                    token_to_channel(normed[2], "ffn_in0", i)
                    token_to_channel(normed[2], "ffn_in1", i)
                later_windows(0)
                if attend:
                    eng.wait_ge(feature_ready, 3 * (i - LAG_ATTEND) + 3)
                    scores(0, "early")
                up(0, 1)
                later_windows(1)
                if attend:
                    scores(0, "late")
                up(2, 3)
                if attend:
                    scores(1, "early")
                later_windows(2)
                if features:
                    g = i - LAG_FEATURES
                    if isinstance(g, int) and g == 0:
                        eng.wait_ge(s_weights_ready, 3)
                        eng.wait_ge(s_loads, 16 * LOADS)
                    eng.wait_ge(normed_ready[1], g + 1)
                    token_to_channel(normed[1], "attn_in0", i)
                    token_to_channel(normed[1], "attn_in1", i)
                if attend:
                    scores(1, "late")
                    retrieve()
                if features:
                    for half in range(2):
                        job = f"hidden{half}"
                        wait_taken(eng, f"attn_in{half}", i)
                        wait_free(eng, job, i)
                        two_parts(bank[BANK_OF[job]][:, :], kq_hi[:, :], kq_lo[:, :],
                                  normed_t[1][:, half * HALF:(half + 1) * HALF])\
                            .then_inc(full[BANK_OF[job]], 1)
                later_windows(3)
                if attend:
                    wait_taken(eng, "retrieved", i)
                    channel_to_token(retrieved, "retrieved_tok", i)
                if ffn:
                    wait_taken(eng, "up3", i)
                    by_halves("gate", lambda k: gate_w[:, k, :], lambda k: act[:, k, :], i, (P, P))
                later_windows(4, 5)
                if ffn:
                    wait_taken(eng, "gate", i)
                    channel_to_token(logits_ch, "gate_tok", i)
                values(0)
                later_windows(6, 7)
                values(1)
                experts(0)
                later_windows(8, 9)
                experts(1)
                if ffn:
                    eng.wait_ge(weight_ready, i - LAG_FFN + 1)
                    wait_free(eng, "weights_ch", i)
                    T.transpose(bank[3][:, 0:P], weight[:, :, :].rearrange("p t e -> p (t e)"),
                                ident[:, :]).then_inc(full[3], 1)
                experts(2)
                if features:
                    wait_taken(eng, "hidden1", i)
                    by_halves("phase_k", lambda k: phase_k_w[:, :], lambda k: hidden[:, :], i)
                    by_halves("phase_q", lambda k: phase_q_w[:, :], lambda k: hidden[:, :], i)
                if ffn:
                    wait_taken(eng, "weights_ch", i)
                    wait_free(eng, "down_bias", i)
                    T.matmul(bank[2][:, :], weight_ch[:, :], down_b[:, :], start=True, stop=True)\
                        .then_inc(full[2], 1)
                experts(3, 4)
                if conv:
                    if isinstance(i, int) and i == 0:
                        eng.wait_ge(s_conv_ready, 1)
                    wait_taken(eng, "window8", i)
                    wait_taken(eng, "window9", i)
                    by_halves("conv", lambda k: conv_wt[:, k, :], lambda k: window_t[:, k, :], i,
                              (P,) * (BLOCKS - 1) + (TAIL,))
                experts(5)
                if conv:
                    wait_taken(eng, "conv", i)
                    channel_to_token(conv_ch, "conv_tok", i)
                experts(6, 7)

            emit(body)(pe)

    return nc


def kernel(**inputs):
    import numpy as _np
    import concourse.bacc as _bacc
    from concourse import mybir as _mybir
    from concourse.bass_utils import run_bass_kernel_spmd as _run

    def t(name):
        return _np.ascontiguousarray(_np.transpose(_np.asarray(inputs[name])))

    def plain(name):
        return _np.ascontiguousarray(_np.asarray(inputs[name]))

    conv_w = _np.asarray(inputs["L0_tok_W"])
    arrays = {
        "x": plain("x").reshape(-1),
        "emb": plain("L0_tok_emb"),
        "conv_w": _np.ascontiguousarray(_np.transpose(conv_w, (2, 1, 0))).reshape(WINDOW, D),
        "conv_b": plain("L0_tok_b"),
        "kw1": t("L0_attn_kw1"), "kb1": plain("L0_attn_kb1"), "kw2": t("L0_attn_kw2"), "kb2": plain("L0_attn_kb2"),
        "qw1": t("L0_attn_qw1"), "qb1": plain("L0_attn_qb1"), "qw2": t("L0_attn_qw2"), "qb2": plain("L0_attn_qb2"),
        "vw": t("L0_attn_vw"), "vb": plain("L0_attn_vb"),
        "w1": plain("L0_ffn_W1"), "b1": plain("L0_ffn_b1"), "wg": plain("L0_ffn_Wg"), "bg": plain("L0_ffn_bg"),
        "wd": plain("L0_ffn_Wd"), "bd": plain("L0_ffn_bd"),
    }
    nc = _bacc.Bacc("TRN2", target_bir_lowering=False, num_devices=1)
    args = [nc.dram_tensor(f"in_{n}", a.shape, _mybir.dt.from_np(a.dtype), kind="ExternalInput").ap()
            for n, a in arrays.items()]
    out = nc.dram_tensor("out_h", (TOKENS, D), _mybir.dt.float32, kind="ExternalOutput").ap()
    build(nc, *args, out)
    r = _run(nc, [{f"in_{n}": a for n, a in arrays.items()}], core_ids=[0])
    return r.results[0]["out_h"].reshape(BATCH, SEQ, D)
```

```python
import numpy as np
import concourse.bass as bass
from concourse import mybir
from contextlib import ExitStack

fp32 = mybir.dt.float32
fp32r = mybir.dt.float32r
int32 = mybir.dt.int32
ALU = mybir.AluOpType
ACT = mybir.ActivationFunctionType
AX = mybir.AxisListType.X

P = 128
BATCH, SEQ = 64, 256
D = 64
VOCAB, KSIZE = 50257, 9
REACH = KSIZE // 2
PHASES = 32
HIDDEN, EXPERTS = 256, 8
EPS = 1e-5

TOKENS = BATCH * SEQ
TILES = TOKENS // P
GT = 8
GROUPS = TILES // GT
HALF = GT // 2 * P
WINDOW = KSIZE * D
BLOCKS = (WINDOW + P - 1) // P
EDGE = 2 * REACH
LAST_START = VOCAB - KSIZE
WIN_COLS = WINDOW + 2 * EDGE + 1
TAIL = WIN_COLS - (BLOCKS - 1) * P
QUADRANT = 32
PI_BELOW = float(np.nextafter(np.float32(np.pi), np.float32(0)))

LAG_CONV, LAG_FEATURES, LAG_ATTEND, LAG_FFN = 0, 1, 2, 3

BANK_JOBS = {
    0: [("window0", 0), ("window2", 0), ("window4", 0), ("window6", 0), ("window8", 0)],
    1: [("window1", 0), ("window3", 0), ("window5", 0), ("window7", 0), ("window9", 0)],
    2: [("retrieved", 2), ("down_bias", 3), ("conv", 0)],
    3: [("retrieved_tok", 2), ("weights_ch", 3), ("conv_tok", 0)],
    4: [("ffn_in0", 3), ("up0", 3), ("up2", 3), ("attn_in0", 1), ("gate", 3), ("hidden0", 1), ("value0", 1),
        ("phase_k", 1)],
    5: [("ffn_in1", 3), ("up1", 3), ("up3", 3), ("attn_in1", 1), ("hidden1", 1), ("gate_tok", 3), ("value1", 1),
        ("phase_q", 1)],
    6: [("scores0_early", 2), ("scores1_early", 2), ("expert0", 3), ("expert2", 3), ("expert4", 3), ("expert6", 3)],
    7: [("scores0_late", 2), ("scores1_late", 2), ("expert1", 3), ("expert3", 3), ("expert5", 3), ("expert7", 3)],
}
BANK_OF = {job: bank for bank, jobs in BANK_JOBS.items() for job, _ in jobs}


def jobs_before(job, i, groups):
    jobs = BANK_JOBS[BANK_OF[job]]
    count, reached = 0, False
    for name, lag in jobs:
        reached = reached or name == job
        if isinstance(i, int):
            count += min(max(i - lag, 0), groups)
            if not reached and 0 <= i - lag < groups:
                count += 1
        else:
            count += -lag + (0 if reached else 1)
    return count if isinstance(i, int) else i * len(jobs) + count


class Chain:

    def __init__(self, engine, sem, group, steps, done=0):
        self.engine, self.sem, self.base, self.steps, self.n = engine, sem, group * steps, steps, done

    def __call__(self, instruction):
        self.n += 1
        instruction.then_inc(self.sem, 1)
        self.engine.wait_ge(self.sem, self.base + self.n)

    def skip(self):
        self.n += 1
        self.engine.wait_ge(self.sem, self.base + self.n)

    def end(self):
        assert self.n == self.steps


def over_last(ap, n):
    return ap.unsqueeze(2).broadcast_to([ap.shape[0], ap.shape[1], n])


def build(nc, x, emb, conv_w, conv_b, kw1, kb1, kw2, kb2, qw1, qb1, qw2, qb2, vw, vb,
          w1, b1, wg, bg, wd, bd, out, groups=GROUPS):
    iterations = groups + LAG_FFN
    tiles = groups * GT
    with ExitStack() as ctx:
        def sb(name, shape, dt=fp32):
            return ctx.enter_context(nc.sbuf_tensor(name, shape, dt))

        def sem(name):
            return ctx.enter_context(nc.semaphore(name))

        ident = sb("ident", [P, P])
        mask = sb("mask", [P, 3 * P])
        priority = sb("priority", [P, EXPERTS])
        edge_ids = sb("edge_ids", [P, 2 * EDGE])
        conv_wt = sb("conv_wt", [P, BLOCKS, D])
        edge_rows = sb("edge_rows", [2 * (EDGE + KSIZE), D])
        edge_cols = sb("edge_cols", [D, 2 * (EDGE + KSIZE)])
        kq_hi = sb("kq_hi", [P, P], fp32r)
        kq_lo = sb("kq_lo", [P, P], fp32r)
        v_raw = sb("v_raw", [P, 3 * D])
        v_parts = sb("v_parts", [P, 4 * D], fp32r)
        up_hi = sb("up_hi", [P, HIDDEN], fp32r)
        up_lo = sb("up_lo", [P, HIDDEN], fp32r)
        down_hi = sb("down_hi", [P, 2, EXPERTS * D], fp32r)
        down_lo = sb("down_lo", [P, 2, EXPERTS * D], fp32r)
        phase_k_w = sb("phase_k_w", [P, D])
        phase_q_w = sb("phase_q_w", [P, D])
        gate_w = sb("gate_w", [P, 2, QUADRANT])
        down_b_hi = sb("down_b_hi", [P, GT * D], fp32r)
        down_b_lo = sb("down_b_lo", [P, GT * D], fp32r)
        hidden_b = sb("hidden_b", [P, 1])
        phase_k_b = sb("phase_k_b", [P, 1])
        phase_q_b = sb("phase_q_b", [P, 1])
        v_b = sb("v_b", [P, D])
        up_b = sb("up_b", [P, 2])
        gate_b = sb("gate_b", [P, 1])
        fold = sb("fold", [P, 1])
        sin_scale = sb("sin_scale", [P, 1])
        sin_shift = sb("sin_shift", [P, 1])
        minus_half = sb("minus_half", [P, GT])

        x_rows = sb("x_rows", [P, P], int32)
        x_edge = sb("x_edge", [P, TILES])
        x_start = sb("x_start", [P, TILES], int32)
        start8 = sb("start8", [P, GT], int32)

        h_all = sb("h_all", [P, TILES, D])
        window = sb("window", [P, GT, WIN_COLS])
        window_t = sb("window_t", [P, BLOCKS, GT * P])
        conv_ch = sb("conv_ch", [P, HALF])
        sums = {s: sb(f"sums{s}", [P, GT]) for s in (1, 2)}
        neg_mean = {s: sb(f"neg_mean{s}", [P, GT]) for s in (1, 2)}
        variance = {s: sb(f"variance{s}", [P, GT]) for s in (1, 2)}
        rstd = {s: sb(f"rstd{s}", [P, GT]) for s in (1, 2)}
        centred = {s: sb(f"centred{s}", [P, GT, D]) for s in (1, 2)}
        scaled = sb("scaled", [P, GT, D])
        normed = {s: sb(f"normed{s}", [P, GT, 2, D]) for s in (1, 2)}
        squares = {s: normed[s][:, :, 0, :] for s in (1, 2)}
        normed_t = {s: sb(f"normed_t{s}", [P, GT * P], fp32r) for s in (1, 2)}
        hidden = sb("hidden", [P, GT * P])
        turn = {s: sb(f"turn_{s}", [P, HALF]) for s in "kq"}
        folded = {s: sb(f"folded_{s}", [P, HALF]) for s in "kq"}
        feature = turn
        key_hi, key_lo = (sb(f"key_{part}", [P, HALF], fp32r) for part in ("hi", "lo"))
        query_hi, query_lo = (sb(f"query_{part}", [P, 2, HALF], fp32r) for part in ("hi", "lo"))
        value_hi = sb("value_hi", [P, GT, D])
        value = sb("value", [P, GT, D])
        attn = sb("attn", [P, 2, 2, 3 * P])
        retrieved = sb("retrieved", [P, HALF])
        act = sb("act", [P, 2, GT * P])
        act_hi = sb("act_hi", [P, 2, GT * P], fp32r)
        act_lo = sb("act_lo", [P, 2, GT * P], fp32r)
        logits_ch = sb("logits_ch", [P, HALF])
        logits = sb("logits", [P, GT, EXPERTS])
        top = sb("top", [P, GT])
        below = sb("below", [P, GT, EXPERTS])
        ranked = sb("ranked", [P, GT, EXPERTS])
        first = sb("first", [P, GT])
        chosen = sb("chosen", [P, GT, EXPERTS])
        exps = sb("exps", [P, GT, EXPERTS])
        total = sb("total", [P, GT])
        top_prob = sb("top_prob", [P, GT])
        weight = sb("weight", [P, GT, EXPERTS])
        weight_parts = sb("weight_parts", [P, 2, GT, EXPERTS])
        weight_ch = sb("weight_ch", [P, P], fp32r)
        picked = sb("picked", [P, GT, EXPERTS * D])
        down_raw = picked[:, 0:2, :]
        down_b_raw = picked[:, 2, :]
        norm = picked[:, 3, 0:3 * P]
        conv_rows = picked[0:D, 4:6, :].rearrange("p t c -> p (t c)")[:, 0:KSIZE * D]\
            .rearrange("p (k o) -> p k o", k=KSIZE)
        edge_diff = picked[0:D, 6, 0:KSIZE * 2 * EDGE].rearrange("p (k e) -> p k e", k=KSIZE)
        x_start_f = picked[:, 6, 2 * P:2 * P + TILES]
        kq_raw = picked[:, 7, 0:P]
        up_raw = picked[:, 7, P:P + HIDDEN]
        x_float = picked[:, 7, P + HIDDEN:2 * P + HIDDEN]
        add4 = sb("add4", [P, 2, 4 * D])
        add2 = sb("add2", [P, 2, 2 * D])
        expert_out = sb("expert_out", [P, GT, D])
        base = sb("base", [P, GT, D])
        result = sb("result", [P, GT, D])
        carrier = sb("carrier", [P, 1])
        carried = sb("carried", [P, 1])
        warm = sb("warm", [P, 1])
        zero = sb("zero", [P, 1])

        bank = [ctx.enter_context(nc.psum_tensor(f"bank{b}", [P, 512], fp32)) for b in range(8)]
        full = [sem(f"bank{b}_full") for b in range(8)]
        free = [sem(f"bank{b}_free") for b in range(8)]

        s_x = sem("s_x")
        s_conv_w = sem("s_conv_w")
        s_edge_rows = sem("s_edge_rows")
        s_feature_loads = sem("s_feature_loads")
        s_ffn_loads = sem("s_ffn_loads")
        s_const = sem("s_const")
        s_row_const = sem("s_row_const")
        s_ident = sem("s_ident")
        s_query_zero = sem("s_query_zero")
        s_zero = sem("s_zero")
        s_norm = sem("s_norm")
        s_sqrt = sem("s_sqrt")
        s_setup_pe = sem("s_setup_pe")
        s_x_float = sem("s_x_float")
        s_edge_cols = sem("s_edge_cols")
        s_edge_diff = sem("s_edge_diff")
        s_conv_ready = sem("s_conv_ready")
        s_weights_ready = sem("s_weights_ready")
        gathered = [sem(f"gathered{h}") for h in range(2)]
        gather_ready = sem("gather_ready")
        window_cols = sem("window_cols")
        rstd_ready = {s: sem(f"rstd_ready{s}") for s in (1, 2)}
        normed_ready = {s: sem(f"normed_ready{s}") for s in (1, 2)}
        folded_ready = sem("folded_ready")
        sine_ready = sem("sine_ready")
        feature_hi_ready = sem("feature_hi_ready")
        feature_ready = sem("feature_ready")
        split_hi = sem("split_hi")
        value_part = sem("value_part")
        wait_carried = sem("wait_carried")
        split_ready = sem("split_ready")
        expert_sum = sem("expert_sum")
        ranked_ready = sem("ranked_ready")
        exps_ready = sem("exps_ready")
        weight_split = sem("weight_split")
        weight_ready = sem("weight_ready")
        result_ready = sem("result_ready")
        stored = sem("stored")
        chain_ln = {s: sem(f"chain_ln{s}") for s in (1, 2)}
        chain_soft = sem("chain_soft")
        chain_adds = sem("chain_adds")
        chain_setup = sem("chain_setup")

        LN_STEPS, SOFT_STEPS, ADD_STEPS, SETUP_STEPS = 8, 7, 8, 11
        ZEROED, CONSTS_EARLY, CONSTS, FEATURE_LOADS, FFN_LOADS = 6, 6, 8, 21, 25

        block = ctx.enter_context(nc.Block())

        def emit(body):
            def program(eng):
                lead = LAG_FFN + 1
                for i in range(lead):
                    body(eng, i)
                if groups - 1 > lead:
                    with eng.Fori(lead, groups - 1) as i:
                        body(eng, i)
                for i in range(max(groups - 1, lead), iterations):
                    body(eng, i)
            return program

        def runs(i, lag):
            return not isinstance(i, int) or 0 <= i - lag < groups

        def filling(i):
            return isinstance(i, int) and i < LAG_FFN

        def early(i):
            return isinstance(i, int) and i == LAG_FEATURES

        def wait_full(eng, job, i):
            eng.wait_ge(full[BANK_OF[job]], jobs_before(job, i, groups) + 1)

        def wait_free(eng, job, i):
            n = jobs_before(job, i, groups)
            if not isinstance(n, int) or n > 0:
                eng.wait_ge(free[BANK_OF[job]], n)

        def wait_taken(eng, job, i):
            eng.wait_ge(free[BANK_OF[job]], jobs_before(job, i, groups) + 1)

        def tiles_of(ap, g):
            return ap[:, bass.ds(g * GT, GT), :]

        def by_half(b):
            return bank[b][:, :].rearrange("p (s h d) -> p h s d", h=2, d=D)

        @block.sync
        def _(sp):
            n_rows = tiles
            sp.dma_start(x_rows[0:n_rows, :], x.rearrange("(t p) -> t p", p=P)[0:n_rows, :]).then_inc(s_x, 16)
            k = EDGE + KSIZE
            sp.dma_start(edge_rows[0:EDGE, :], emb[0:1, :].broadcast_to([EDGE, D])).then_inc(s_edge_rows, 16)
            sp.dma_start(edge_rows[EDGE:k, :], emb[0:KSIZE, :]).then_inc(s_edge_rows, 16)
            sp.dma_start(edge_rows[k:k + KSIZE, :], emb[LAST_START:VOCAB, :]).then_inc(s_edge_rows, 16)
            sp.dma_start(edge_rows[k + KSIZE:2 * k, :],
                         emb[VOCAB - 1:VOCAB, :].broadcast_to([EDGE, D])).then_inc(s_edge_rows, 16)
            whole = (BLOCKS - 1) * P
            sp.dma_start(conv_wt[:, 0:BLOCKS - 1, :],
                         conv_w[0:whole, :].rearrange("(k p) o -> p k o", p=P)).then_inc(s_conv_w, 16)
            sp.dma_start(conv_wt[0:D, BLOCKS - 1, :], conv_w[whole:WINDOW, :]).then_inc(s_conv_w, 16)
            sp.dma_start(conv_wt[TAIL - 1:TAIL, BLOCKS - 1, :],
                         conv_b.rearrange("(a o) -> a o", a=1)).then_inc(s_conv_w, 16)
            sp.dma_start(conv_rows[:, :, :], conv_w.rearrange("(k p) o -> p k o", p=D)).then_inc(s_conv_w, 16)

            sp.wait_ge(s_zero, ZEROED)
            def column(v):
                return v.rearrange("(p a) -> p a", a=1)

            feature_loads = []
            for r in (0, D):
                feature_loads += [(kq_raw[r:r + D, 0:D], kw1), (kq_raw[r:r + D, D:P], qw1), (v_raw[r:r + D, 0:D], vw)]
            for c in (0, PHASES):
                feature_loads += [(phase_k_w[0:D, c:c + PHASES], kw2), (phase_q_w[D:P, c:c + PHASES], qw2)]
            feature_loads += [(hidden_b[0:D, :], column(kb1)), (hidden_b[D:P, :], column(qb1)),
                              (v_b[:, :], vb.rearrange("(a d) -> a d", a=1).broadcast_to([P, D]))]
            for r in range(0, P, PHASES):
                feature_loads += [(phase_k_b[r:r + PHASES, :], column(kb2)), (phase_q_b[r:r + PHASES, :], column(qb2))]
            assert len(feature_loads) == FEATURE_LOADS
            for dst, src in feature_loads:
                sp.dma_start(dst, src).then_inc(s_feature_loads, 16)

            ffn_loads = [(up_raw[0:D, :], w1), (up_raw[D:P, :], w1),
                         (gate_w[:, :, 0:EXPERTS], wg.rearrange("(k p) e -> p k e", p=P)),
                         (gate_b[0:EXPERTS, :], column(bg)), (gate_b[D:D + EXPERTS, :], column(bg)),
                         (up_b[:, 0:1], column(b1[0:P])), (up_b[:, 1:2], column(b1[P:HIDDEN]))]
            wd_v = wd.rearrange("e (k p) d -> k p e d", p=P)
            for c in range(2):
                ffn_loads += [(down_raw[:, c, :].rearrange("p (e d) -> p e d", e=EXPERTS), wd_v[c])]
            for part in range(2):
                for t in range(GT):
                    row = (part * GT + t) * EXPERTS
                    ffn_loads += [(down_b_raw[row:row + EXPERTS, t * D:(t + 1) * D], bd)]
            assert len(ffn_loads) == FFN_LOADS
            for dst, src in ffn_loads:
                sp.dma_start(dst, src).then_inc(s_ffn_loads, 16)

            def store(eng, i):
                if runs(i, LAG_FFN):
                    g = i - LAG_FFN
                    eng.wait_ge(result_ready, g + 1)
                    dst = out.rearrange("(t p) d -> p t d", p=P)[:, bass.ds(g * GT, GT), :]
                    eng.dma_start(dst, result[:, :, :]).then_inc(stored, 16)

            emit(store)(sp)
            sp.wait_ge(stored, 16 * groups)

        @block.gpsimd
        def _(pool):
            G = nc.gpsimd
            G.memset(ident[:, :], 0.0).then_inc(s_ident, 1)
            pool.wait_ge(s_ident, 1)
            G.affine_select(out=ident[:, :], in_=ident[:, :], compare_op=ALU.not_equal, fill=1.0, base=0,
                            pattern=[[-1, P]], channel_multiplier=1).then_inc(s_ident, 1)
            for ap in (v_raw[:, :], phase_k_w[:, :], phase_q_w[:, :], gate_w[:, :, :], gate_b[:, :], down_b_raw):
                G.memset(ap, 0.0).then_inc(s_zero, 1)
            G.iota(edge_ids[:, 0:EDGE], pattern=[[1, EDGE]], base=-REACH, channel_multiplier=0,
                   allow_small_or_imprecise_dtypes=True).then_inc(s_const, 1)
            G.iota(edge_ids[:, EDGE:2 * EDGE], pattern=[[1, EDGE]], base=VOCAB - REACH, channel_multiplier=0,
                   allow_small_or_imprecise_dtypes=True).then_inc(s_const, 1)
            G.iota(priority[:, :], pattern=[[-1, EXPERTS]], base=EXPERTS, channel_multiplier=0,
                   allow_small_or_imprecise_dtypes=True).then_inc(s_const, 1)
            G.memset(window[:, :, WIN_COLS - 1:WIN_COLS], 1.0).then_inc(s_const, 1)
            G.memset(minus_half[:, :], -0.5).then_inc(s_const, 1)
            G.memset(zero[:, :], 0.0).then_inc(s_const, 1)
            G.iota(norm, pattern=[[PHASES, 3 * P]], base=PHASES, channel_multiplier=0,
                   allow_small_or_imprecise_dtypes=True).then_inc(s_norm, 1)
            pool.wait_ge(s_norm, 1)
            G.iota(norm[:, 2 * P:3 * P], pattern=[[PHASES, P]], base=PHASES * (P + 1), channel_multiplier=0,
                   allow_small_or_imprecise_dtypes=True).then_inc(s_norm, 1)
            def gather(eng, g, half, i=None):
                if i is not None:
                    wait_full(eng, f"window{BLOCKS * half + BLOCKS - 1}", i)
                    eng.wait_ge(gather_ready, g + 1)
                    if not isinstance(g, int) or g > 1 or half > 0:
                        eng.wait_ge(wait_carried, 2 * (g - 1) + half)
                    G.tensor_tensor(carrier[:, :], minus_half[:, 0:1], minus_half[:, 0:1], ALU.add)\
                        .then_inc(wait_carried, 1)
                for t in range(4 * half, 4 * half + 4):
                    eng.indirect_dma_start(
                        out=window[:, t, 0:WINDOW], out_offset=None, in_=emb,
                        in_offset=bass.IndirectOffsetOnAxis(ap=start8[:, t:t + 1], axis=0),
                    ).then_inc(gathered[half], 16)

            pool.wait_ge(gather_ready, 1)
            gather(pool, 0, 0)
            gather(pool, 0, 1)
            pool.wait_ge(s_norm, 3)
            G.affine_select(out=mask[:, 0:2 * P], in_=mask[:, 0:2 * P], compare_op=ALU.is_ge, fill=0.0, base=0,
                            pattern=[[1, 2 * P]], channel_multiplier=-1).then_inc(s_const, 1)
            G.affine_select(out=mask[:, 2 * P:3 * P], in_=mask[:, 2 * P:3 * P], compare_op=ALU.is_ge, fill=0.0,
                            base=0, pattern=[[1, P]], channel_multiplier=-1).then_inc(s_const, 1)

            def inverse_root(eng, s, g):
                eng.wait_ge(chain_ln[s], g * LN_STEPS + 6)
                G.tensor_tensor(rstd[s][:, :], variance[s][:, :], minus_half[:, :], ALU.pow)\
                    .then_inc(rstd_ready[s], 1)

            def body(eng, i):
                attend, ffn, more = runs(i, LAG_ATTEND), runs(i, LAG_FFN), runs(i + 1, LAG_CONV)
                g = i - LAG_FFN
                chain = Chain(eng, chain_adds, g, ADD_STEPS)

                def add_pair(pair, before_last=None):
                    two = slice(2 * pair, 2 * pair + 2)
                    wait_taken(eng, f"expert{2 * pair + 1}", i)
                    chain(G.tensor_tensor(add4[:, :, :], picked[:, two, 0:4 * D], picked[:, two, 4 * D:8 * D],
                                          ALU.add))
                    chain(G.tensor_tensor(add2[:, :, :], add4[:, :, 0:2 * D], add4[:, :, 2 * D:4 * D], ALU.add))
                    last = G.tensor_tensor(expert_out[:, two, :], add2[:, :, 0:D], add2[:, :, D:2 * D], ALU.add)
                    if pair == GT // 2 - 1:
                        last.then_inc(expert_sum, 1)

                if more:
                    gather(eng, i + 1, 0, i)
                if attend:
                    inverse_root(eng, 2, i - LAG_ATTEND)
                if more:
                    gather(eng, i + 1, 1, i)
                if runs(i, LAG_FEATURES):
                    eng.wait_ge(feature_hi_ready, 3 * (i - LAG_FEATURES) + 1)
                    G.tensor_tensor(key_lo[:, :], feature["k"][:, :], key_hi[:, :].bitcast(fp32), ALU.subtract)\
                        .then_inc(feature_ready, 1)
                if ffn:
                    add_pair(0)
                    add_pair(1)
                if runs(i, LAG_CONV):
                    inverse_root(eng, 1, i)
                if ffn:
                    add_pair(2)
                    add_pair(3)
                    chain.end()
                    eng.wait_ge(expert_sum, g + 1)
                    wait_taken(eng, "down_bias", i)
                    if not isinstance(g, int) or g > 0:
                        eng.wait_ge(stored, 16 * g)
                    G.tensor_tensor(result[:, :, :], expert_out[:, :, :], base[:, :, :], ALU.add)\
                        .then_inc(result_ready, 1)

            emit(body)(pool)

        @block.scalar
        def _(sc):
            S = nc.scalar
            sc.wait_ge(s_norm, 2)
            S.activation(norm, norm, ACT.Sqrt).then_inc(s_sqrt, 1)
            sc.wait_ge(s_edge_cols, 1)
            S.activation(edge_cols[:, :], bank[7][0:D, 0:2 * (EDGE + KSIZE)], ACT.Copy).then_inc(s_edge_cols, 1)
            sc.wait_ge(s_row_const, 12)

            def copy_out(eng, dst, job, i):
                wait_full(eng, job, i)
                S.activation(dst, bank[BANK_OF[job]][:, :], ACT.Copy).then_inc(free[BANK_OF[job]], 1)

            def copy_window(eng, n, i):
                half, k = divmod(n, BLOCKS)
                rows = P if k < BLOCKS - 1 else TAIL
                job = f"window{n}"
                wait_full(eng, job, i)
                S.activation(window_t[0:rows, k, half * HALF:(half + 1) * HALF], bank[BANK_OF[job]][0:rows, :],
                             ACT.Copy).then_inc(free[BANK_OF[job]], 1)

            def body(eng, i):
                conv, features, attend, ffn = (runs(i, lag) for lag in
                                               (LAG_CONV, LAG_FEATURES, LAG_ATTEND, LAG_FFN))

                def halves(ap, half):
                    return ap[:, half * HALF:(half + 1) * HALF]

                def windows(*which):
                    for n in which:
                        if conv:
                            copy_window(eng, n, i)

                def later_windows(*which):
                    if not filling(i):
                        windows(*which)

                def square(s, g):
                    eng.wait_ge(chain_ln[s], g * LN_STEPS + 3)
                    S.activation(squares[s], centred[s][:, :, :], ACT.Square).then_inc(chain_ln[s], 1)

                def copy_residual():
                    wait_full(eng, "conv_tok", i)
                    S.activation(tiles_of(h_all, i).rearrange("p (h s) d -> p h s d", h=2), by_half(3),
                                 ACT.Copy).then_inc(free[3], 1)

                def tanh(half):
                    if features:
                        job = f"hidden{half}"
                        wait_full(eng, job, i)
                        S.activation(halves(hidden, half), bank[BANK_OF[job]][:, :],
                                     ACT.Tanh, bias=hidden_b[:, 0:1]).then_inc(free[BANK_OF[job]], 1)

                if isinstance(i, int) and i == LAG_FEATURES:
                    eng.wait_ge(s_feature_loads, 16 * FEATURE_LOADS)
                if isinstance(i, int) and i == LAG_FFN:
                    eng.wait_ge(s_ffn_loads, 16 * FFN_LOADS)
                if filling(i):
                    if not early(i - 1):
                        windows(0, 1, 2, 3)
                    if i == 1:
                        square(1, 0)
                    windows(4, 5, 6, 7, 8, 9)
                if early(i):
                    copy_out(eng, conv_ch[:, :], "conv", i)
                if ffn:
                    g = i - LAG_FFN
                    for half in range(2):
                        copy_out(eng, halves(normed_t[2], half), f"ffn_in{half}", i)
                if ffn:
                    for n in range(4):
                        half, part = divmod(n, 2)
                        job = f"up{n}"
                        if n == 2:
                            later_windows(0, 1)
                        wait_full(eng, job, i)
                        S.activation(act[:, part, half * HALF:(half + 1) * HALF], bank[BANK_OF[job]][:, :],
                                     ACT.Gelu, bias=up_b[:, part:part + 1]).then_inc(free[BANK_OF[job]], 1)
                else:
                    later_windows(0, 1)
                later_windows(2)
                if features:
                    for half in range(2):
                        copy_out(eng, halves(normed_t[1], half), f"attn_in{half}", i)
                if early(i):
                    copy_residual()
                if ffn:
                    S.activation(warm[:, :], sin_shift[:, :], ACT.Exp)
                if attend:
                    copy_out(eng, retrieved[:, :], "retrieved", i)
                if ffn:
                    wait_full(eng, "gate", i)
                    S.activation(logits_ch[:, :], bank[4][:, :], ACT.Identity, bias=gate_b[:, 0:1])\
                        .then_inc(free[4], 1)
                tanh(1)
                later_windows(3)
                tanh(0)
                later_windows(4, 5)
                if ffn:
                    eng.wait_ge(chain_soft, g * SOFT_STEPS + 2)
                    S.activation(exps[:, :, :], below[:, :, :], ACT.Exp).then_inc(exps_ready, 1)
                later_windows(6, 7, 8, 9)
                if ffn:
                    wait_full(eng, "weights_ch", i)
                    S.activation(weight_ch[:, :], bank[3][:, 0:P], ACT.Copy).then_inc(free[3], 1)
                if attend:
                    square(2, i - LAG_ATTEND)
                if early(i):
                    square(1, i)
                if features:
                    for s, bias in (("k", phase_k_b), ("q", phase_q_b)):
                        job = f"phase_{s}"
                        wait_full(eng, job, i)
                        S.activation(turn[s][:, :], bank[BANK_OF[job]][:, :], ACT.Tanh, bias=bias[:, 0:1])\
                            .then_inc(free[BANK_OF[job]], 1)
                    for n, s in enumerate("kq"):
                        eng.wait_ge(folded_ready, 2 * (i - LAG_FEATURES) + n + 1)
                        S.activation(feature[s][:, :], folded[s][:, :], ACT.Sin, scale=sin_scale[:, 0:1],
                                     bias=sin_shift[:, 0:1]).then_inc(sine_ready, 1)
                if not filling(i + 1):
                    S.activation(warm[:, :], sin_shift[:, :], ACT.Gelu)
                if conv and not early(i):
                    copy_out(eng, conv_ch[:, :], "conv", i)
                    copy_residual()
                    if not isinstance(i, int) or i > 0:
                        square(1, i)

            emit(body)(sc)

        @block.vector
        def _(dve):
            V = nc.vector
            link = Chain(dve, chain_setup, 0, SETUP_STEPS)
            for q in range(4):
                rows = slice(32 * q, 32 * q + 32)
                cosine = q % 2 == 0
                V.memset(fold[rows, :], -1.0 if cosine else 1.0).then_inc(s_row_const, 1)
                V.memset(sin_scale[rows, :], -PI_BELOW if cosine else PI_BELOW).then_inc(s_row_const, 1)
                V.memset(sin_shift[rows, :], float(np.pi / 2) if cosine else 0.0).then_inc(s_row_const, 1)
            dve.wait_ge(s_x, 16)
            V.tensor_copy(x_float[0:tiles, :], x_rows[0:tiles, :]).then_inc(s_x_float, 1)
            dve.wait_ge(s_x_float, 1)
            link(V.tensor_scalar(x_float[0:tiles, :], x_float[0:tiles, :], float(-REACH),
                                 float(VOCAB + REACH - 1), ALU.max, ALU.min))
            dve.wait_ge(s_setup_pe, 1)
            link(V.tensor_copy(x_edge[:, 0:tiles], bank[6][:, 0:tiles]))
            link(V.tensor_scalar(x_start_f[:, 0:tiles], x_edge[:, 0:tiles], float(-REACH), 0.0, ALU.add, ALU.max))
            link(V.tensor_scalar(x_start_f[:, 0:tiles], x_start_f[:, 0:tiles], float(LAST_START), None, ALU.min))
            link(V.tensor_copy(x_start[:, 0:tiles], x_start_f[:, 0:tiles]))

            def prepare_starts(g):
                V.tensor_copy(start8[:, :], x_start[:, bass.ds(g * GT, GT)]).then_inc(gather_ready, 1)

            def prepare_edges(g):
                V.tensor_tensor(window[:, :, WINDOW:WINDOW + 2 * EDGE],
                                over_last(x_edge[:, bass.ds(g * GT, GT)], 2 * EDGE),
                                edge_ids[:, :].unsqueeze(1).broadcast_to([P, GT, 2 * EDGE]),
                                ALU.is_equal).then_inc(window_cols, 1)

            prepare_starts(0)
            dve.wait_ge(s_const, CONSTS_EARLY)
            prepare_edges(0)
            dve.wait_ge(s_sqrt, 1)
            V.reciprocal(mask[:, :], norm).then_inc(s_norm, 1)
            dve.wait_ge(s_edge_cols, 2)
            k = EDGE + KSIZE
            for j in range(KSIZE):
                V.tensor_tensor(edge_diff[:, j, 0:EDGE], edge_cols[:, j:j + EDGE],
                                edge_cols[:, EDGE + j:EDGE + j + 1].broadcast_to([D, EDGE]),
                                ALU.subtract).then_inc(s_edge_diff, 1)
                V.tensor_tensor(edge_diff[:, j, EDGE:2 * EDGE], edge_cols[:, k + 1 + j:k + 1 + j + EDGE],
                                edge_cols[:, k + j:k + j + 1].broadcast_to([D, EDGE]),
                                ALU.subtract).then_inc(s_edge_diff, 1)
            dve.wait_ge(s_setup_pe, 3)
            V.tensor_copy(conv_wt[D:D + 2 * EDGE, BLOCKS - 1, :], bank[6][D:D + 2 * EDGE, 0:D])\
                .then_inc(s_conv_ready, 1)
            dve.wait_ge(s_const, CONSTS)
            dve.wait_ge(s_row_const, 12)
            for query in (query_hi, query_lo):
                V.tensor_copy(query[:, :, :], over_last(zero[:, :].broadcast_to([P, 2]), HALF)).then_inc(s_query_zero, 1)
            dve.wait_ge(s_query_zero, 2)

            def split_feature_weights():
                dve.wait_ge(s_feature_loads, 16 * FEATURE_LOADS)
                link(V.tensor_copy(kq_hi[:, :], kq_raw[:, :]))
                V.tensor_tensor(kq_lo[:, :], kq_raw[:, :], kq_hi[:, :].bitcast(fp32), ALU.subtract)\
                    .then_inc(s_weights_ready, 1)
                link(V.tensor_copy(v_parts[:, 0:D], v_raw[:, 0:D]))
                V.tensor_copy(v_parts[:, 2 * D:4 * D], v_raw[:, D:3 * D]).then_inc(s_weights_ready, 1)
                V.tensor_tensor(v_parts[:, D:2 * D], v_raw[:, 0:D], v_parts[:, 0:D].bitcast(fp32), ALU.subtract)\
                    .then_inc(s_weights_ready, 1)

            def split_ffn_weights():
                dve.wait_ge(s_ffn_loads, 16 * FFN_LOADS)
                link(V.tensor_copy(up_hi[:, :], up_raw[:, :]))
                V.tensor_tensor(up_lo[:, :], up_raw[:, :], up_hi[:, :].bitcast(fp32), ALU.subtract)\
                    .then_inc(s_weights_ready, 1)
                for c in range(2):
                    link(V.tensor_copy(down_hi[:, c, :], down_raw[:, c, :]))
                    V.tensor_tensor(down_lo[:, c, :], down_raw[:, c, :], down_hi[:, c, :].bitcast(fp32),
                                    ALU.subtract).then_inc(s_weights_ready, 1)
                link(V.tensor_copy(down_b_hi[:, :], down_b_raw))
                V.tensor_tensor(down_b_lo[:, :], down_b_raw, down_b_hi[:, :].bitcast(fp32),
                                ALU.subtract).then_inc(s_weights_ready, 1)
                link.end()

            def split_features(g):
                dve.wait_ge(sine_ready, 2 * g + 1)
                V.tensor_copy(key_hi[:, :], feature["k"][:, :]).then_inc(feature_hi_ready, 1)
                dve.wait_ge(sine_ready, 2 * g + 2)
                rows = [slice(half * D, (half + 1) * D) for half in range(2)]
                for half in range(2):
                    V.tensor_copy(query_hi[rows[half], half, :], feature["q"][rows[half], :])\
                        .then_inc(feature_hi_ready, 1)
                for half in range(2):
                    dve.wait_ge(feature_hi_ready, 3 * g + half + 2)
                    V.tensor_tensor(query_lo[rows[half], half, :], feature["q"][rows[half], :],
                                    query_hi[rows[half], half, :].bitcast(fp32), ALU.subtract)\
                        .then_inc(feature_ready, 1)

            def norm_centre(eng, s, g):
                chain = Chain(eng, chain_ln[s], g, LN_STEPS)
                h = tiles_of(h_all, g)
                chain(V.tensor_reduce(sums[s][:, :], h, axis=AX, op=ALU.add))
                chain(V.tensor_scalar(neg_mean[s][:, :], sums[s][:, :], -1.0 / D, None, ALU.mult))
                chain(V.tensor_tensor(centred[s][:, :, :], h, over_last(neg_mean[s][:, :], D), ALU.add))
                return chain

            def norm_variance(s, chain):
                chain.skip()
                chain(V.tensor_reduce(sums[s][:, :], squares[s], axis=AX, op=ALU.add))
                chain(V.tensor_scalar(variance[s][:, :], sums[s][:, :], 1.0 / D, EPS, ALU.mult, ALU.add))

            def norm_apply(eng, s, g):
                chain = Chain(eng, chain_ln[s], g, LN_STEPS, done=6)
                eng.wait_ge(rstd_ready[s], g + 1)
                chain(V.tensor_tensor(scaled[:, :, :], centred[s][:, :, :], over_last(rstd[s][:, :], D), ALU.mult))
                hi, lo = normed[s][:, :, 0, :], normed[s][:, :, 1, :]
                chain(V.tensor_copy(hi.bitcast(fp32r), scaled[:, :, :]))
                V.tensor_tensor(lo, scaled[:, :, :], hi, ALU.subtract).then_inc(normed_ready[s], 1)
                chain.end()

            def expert(eng, t, i):
                job = f"expert{t}"
                g = i - LAG_FFN
                if t == 0:
                    eng.wait_ge(weight_ready, g + 1)
                    if not isinstance(g, int) or g > 0:
                        eng.wait_ge(expert_sum, g)
                wait_full(eng, job, i)
                V.tensor_tensor(picked[:, t, :].rearrange("p (e d) -> p e d", e=EXPERTS),
                                bank[BANK_OF[job]][:, :].rearrange("p (e d) -> p e d", e=EXPERTS),
                                over_last(weight[:, t, :], D), ALU.mult).then_inc(free[BANK_OF[job]], 1)

            def body(eng, i):
                conv, features, attend, ffn = (runs(i, lag) for lag in
                                               (LAG_CONV, LAG_FEATURES, LAG_ATTEND, LAG_FFN))

                def picks(*which):
                    for t in which:
                        if ffn:
                            expert(eng, t, i)

                def mask_scores(seq, part):
                    cols, at = (SEQ, 0) if part == "early" else (P, SEQ)
                    job = f"scores{seq}_{part}"
                    b = BANK_OF[job]
                    wait_full(eng, job, i)
                    V.tensor_tensor(attn[:, seq, :, at:at + cols],
                                    bank[b][:, 0:2 * cols].rearrange("p (h c) -> p h c", h=2),
                                    mask[:, at:at + cols].unsqueeze(1).broadcast_to([P, 2, cols]),
                                    ALU.mult).then_inc(free[b], 1)

                def values():
                    if features:
                        for n in range(2):
                            job = f"value{n}"
                            wait_full(eng, job, i)
                            parts = bank[BANK_OF[job]][:, :].rearrange("p (t a d) -> p t a d", t=4, a=2)
                            four = slice(4 * n, 4 * n + 4)
                            V.tensor_tensor(value_hi[:, four, :], parts[:, :, 0, :],
                                            v_b[:, :].unsqueeze(1).broadcast_to([P, 4, D]), ALU.add)\
                                .then_inc(value_part, 1)
                            eng.wait_ge(value_part, 2 * (i - LAG_FEATURES) + n + 1)
                            V.tensor_tensor(value[:, four, :], value_hi[:, four, :], parts[:, :, 1, :], ALU.add)\
                                .then_inc(free[BANK_OF[job]], 1)

                def act_part(ap, n):
                    half, part = divmod(n, 2)
                    return ap[:, part, half * HALF:(half + 1) * HALF]

                def split_high(*which):
                    for n in which:
                        if ffn:
                            wait_taken(eng, f"up{n}", i)
                            V.tensor_copy(act_part(act_hi, n), act_part(act, n)).then_inc(split_hi, 1)

                def split_low(*which):
                    for n in which:
                        if ffn:
                            eng.wait_ge(split_hi, (i - LAG_FFN) * 4 + n + 1)
                            V.tensor_tensor(act_part(act_lo, n), act_part(act, n), act_part(act_hi, n).bitcast(fp32),
                                            ALU.subtract).then_inc(split_ready, 1)

                if early(i - 1):
                    for n in range(4):
                        job = f"window{n}"
                        wait_full(eng, job, i)
                        V.tensor_copy(window_t[:, n, 0:HALF], bank[BANK_OF[job]][:, :]).then_inc(free[BANK_OF[job]], 1)
                    split_features(i - 1 - LAG_FEATURES)
                if attend:
                    mask_scores(0, "early")
                if runs(i + 1, LAG_CONV):
                    eng.wait_ge(gathered[1], 64 * (i + 1))
                    prepare_starts(i + 1)
                if isinstance(i, int) and i == LAG_FEATURES:
                    split_feature_weights()
                if features:
                    norm_apply(eng, 1, i - LAG_FEATURES)
                if isinstance(i, int) and i == LAG_FEATURES:
                    split_ffn_weights()
                if early(i):
                    wait_taken(eng, "conv_tok", i)
                    ln_early = norm_centre(eng, 1, i)
                if attend:
                    mask_scores(0, "late")
                    mask_scores(1, "early")
                    mask_scores(1, "late")
                split_high(0, 1)
                split_low(0)
                split_high(2)
                split_low(1)
                split_high(3)
                split_low(2)
                if attend:
                    wait_full(eng, "retrieved_tok", i)
                    h = tiles_of(h_all, i - LAG_ATTEND).rearrange("p (h s) d -> p h s d", h=2)
                    V.tensor_tensor(h, h, by_half(3), ALU.add).then_inc(free[3], 1)
                    wait_taken(eng, "retrieved_tok", i)
                split_low(3)
                if ffn:
                    g = i - LAG_FFN
                    wait_full(eng, "gate_tok", i)
                    chain = Chain(eng, chain_soft, g, SOFT_STEPS)
                    parts = bank[5][:, :].rearrange("p (s h a q) -> p h s q a", h=2, a=2, q=QUADRANT)
                    V.tensor_reduce(logits[:, :, :].rearrange("p (h s) e -> p h s e", h=2),
                                    parts[:, :, :, 0:EXPERTS, :], axis=AX, op=ALU.add).then_inc(free[5], 1)
                    wait_taken(eng, "gate_tok", i)
                    chain(V.tensor_reduce(top[:, :], logits[:, :, :], axis=AX, op=ALU.max))
                    chain(V.tensor_tensor(below[:, :, :], logits[:, :, :], over_last(top[:, :], EXPERTS), ALU.subtract))
                    V.scalar_tensor_tensor(ranked[:, :, :], below[:, :, :], 0.0,
                                           priority[:, :].unsqueeze(1).broadcast_to([P, GT, EXPERTS]),
                                           ALU.is_equal, ALU.mult).then_inc(ranked_ready, 1)
                if ffn:
                    eng.wait_ge(ranked_ready, g + 1)
                    chain(V.tensor_reduce(first[:, :], ranked[:, :, :], axis=AX, op=ALU.max))
                    chain(V.tensor_tensor(chosen[:, :, :], ranked[:, :, :], over_last(first[:, :], EXPERTS),
                                          ALU.is_equal))
                if ffn:
                    eng.wait_ge(exps_ready, g + 1)
                    chain(V.tensor_reduce(total[:, :], exps[:, :, :], axis=AX, op=ALU.add))
                    chain(V.reciprocal(top_prob[:, :], total[:, :]))
                    V.tensor_tensor(weight[:, :, :], chosen[:, :, :], over_last(top_prob[:, :], EXPERTS),
                                    ALU.mult).then_inc(weight_ready, 1)
                    eng.wait_ge(weight_ready, g + 1)
                    chain(V.tensor_copy(weight_parts[:, 0, :, :].bitcast(fp32r), weight[:, :, :]))
                    V.tensor_tensor(weight_parts[:, 1, :, :], weight[:, :, :], weight_parts[:, 0, :, :],
                                    ALU.subtract).then_inc(weight_split, 1)
                    chain.end()
                if not conv:
                    picks(0)
                if attend:
                    ln = norm_centre(eng, 2, i - LAG_ATTEND)
                if conv:
                    picks(0)
                values()
                if early(i):
                    norm_variance(1, ln_early)
                picks(1, 2)
                if attend:
                    norm_variance(2, ln)
                if runs(i + 1, LAG_CONV):
                    wait_full(eng, "window9", i)
                    prepare_edges(i + 1)
                if ffn:
                    wait_full(eng, "down_bias", i)
                    if not isinstance(g, int) or g > 0:
                        eng.wait_ge(result_ready, g)
                    V.tensor_tensor(base[:, :, :], tiles_of(h_all, g),
                                    bank[2][:, :].rearrange("p (t d) -> p t d", t=GT), ALU.add)\
                        .then_inc(free[2], 1)
                if features:
                    for s in "kq":
                        wait_taken(eng, f"phase_{s}", i)
                        V.scalar_tensor_tensor(folded[s][:, :], turn[s][:, :], fold[:, 0:1], turn[s][:, :],
                                               ALU.mult, ALU.max).then_inc(folded_ready, 1)
                picks(3, 4)
                if attend:
                    norm_apply(eng, 2, i - LAG_ATTEND)
                if not conv:
                    picks(5)
                if features and not early(i):
                    split_features(i - LAG_FEATURES)
                if conv:
                    picks(5)
                if conv and not early(i):
                    wait_taken(eng, "conv_tok", i)
                    V.tensor_copy(carried[:, :], minus_half[:, 0:1])
                    ln = norm_centre(eng, 1, i)
                picks(6)
                if conv and not early(i):
                    norm_variance(1, ln)
                picks(7)

            emit(body)(dve)

        @block.tensor
        def _(pe):
            T = nc.tensor
            pe.wait_ge(s_ident, 2)
            pe.wait_ge(chain_setup, 1)
            T.transpose(bank[6][:, 0:tiles], x_float[0:tiles, :], ident[0:tiles, 0:tiles]).then_inc(s_setup_pe, 1)
            k = 2 * (EDGE + KSIZE)
            pe.wait_ge(s_edge_rows, 64)
            T.transpose(bank[7][0:D, 0:k], edge_rows[:, :], ident[0:k, 0:k]).then_inc(s_edge_cols, 1)
            pe.wait_ge(s_conv_w, 64)
            pe.wait_ge(s_edge_diff, 2 * KSIZE)
            pe.wait_ge(chain_setup, 2)
            for j in range(KSIZE):
                last = T.matmul(bank[6][D:D + 2 * EDGE, 0:D], edge_diff[:, j, :], conv_rows[:, j, :],
                                start=(j == 0), stop=(j == KSIZE - 1))
            last.then_inc(s_setup_pe, 2)

            def token_to_channel(src, job, i):
                half = int(job[-1])
                wait_free(pe, job, i)
                for s in range(4):
                    last = T.transpose(bank[BANK_OF[job]][:, s * P:(s + 1) * P],
                                       src[:, 4 * half + s, :, :].rearrange("p a d -> p (a d)"), ident[:, :])
                last.then_inc(full[BANK_OF[job]], 1)

            def channel_to_token(src, job, i):
                wait_free(pe, job, i)
                for s in range(4):
                    last = T.transpose(bank[BANK_OF[job]][:, s * P:(s + 1) * P], src[:, s * P:(s + 1) * P],
                                       ident[:, :])
                last.then_inc(full[BANK_OF[job]], 1)

            def window_transpose(n, i):
                half, k = divmod(n, BLOCKS)
                if k == 0:
                    pe.wait_ge(gathered[half], 64 * (i + 1))
                if n == 4:
                    pe.wait_ge(window_cols, i + 1)
                job = f"window{n}"
                cols = slice(k * P, min((k + 1) * P, WIN_COLS))
                rows = cols.stop - cols.start
                wait_free(pe, job, i)
                for s in range(4):
                    last = T.transpose(bank[BANK_OF[job]][0:rows, s * P:(s + 1) * P],
                                       window[:, 4 * half + s, cols], ident[:, :])
                last.then_inc(full[BANK_OF[job]], 1)

            def by_halves(job, weights, src, i, k_rows=(P,)):
                b = BANK_OF[job]
                wait_free(pe, job, i)
                for k, rows in enumerate(k_rows):
                    for half in range(2):
                        last = T.matmul(bank[b][half * D:(half + 1) * D, :], weights(k)[0:rows, :],
                                        src(k)[0:rows, half * HALF:(half + 1) * HALF],
                                        start=(k == 0), stop=(k == len(k_rows) - 1))
                last.then_inc(full[b], 1)

            def two_parts(out_ap, hi, lo, src):
                T.matmul(out_ap, hi, src, start=True, stop=False)
                return T.matmul(out_ap, lo, src, start=False, stop=True)

            def expert(t, i):
                job = f"expert{t}"
                b = BANK_OF[job]
                pe.wait_ge(split_ready, (i - LAG_FFN) * 4 + (2 if t < 4 else 4))
                wait_free(pe, job, i)
                cols = slice(t * P, (t + 1) * P)
                products = [(act_hi, down_hi), (act_hi, down_lo), (act_lo, down_hi)]
                for k in range(2):
                    for n, (a, w) in enumerate(products):
                        last = T.matmul(bank[b][:, :], a[:, k, cols], w[:, k, :],
                                        start=(k == 0 and n == 0), stop=(k == 1 and n == 2))
                last.then_inc(full[b], 1)

            def body(eng, i):
                conv, features, attend, ffn = (runs(i, lag) for lag in
                                               (LAG_CONV, LAG_FEATURES, LAG_ATTEND, LAG_FFN))

                def windows(*which):
                    for n in which:
                        if conv:
                            window_transpose(n, i)

                def later_windows(*which):
                    if not filling(i):
                        windows(*which)

                def experts(*which):
                    for t in which:
                        if ffn:
                            expert(t, i)

                def scores(seq, part):
                    if not attend:
                        return
                    if part == "early" and seq == 0:
                        eng.wait_ge(feature_ready, 3 * (i - LAG_ATTEND) + 3)
                    job = f"scores{seq}_{part}"
                    b = BANK_OF[job]
                    first = seq * SEQ + (P if part == "late" else 0)
                    n = (seq + 1) * SEQ - first
                    wait_free(eng, job, i)
                    products = ((key_hi, query_hi), (key_hi, query_lo), (key_lo, query_hi))
                    for m, (key, query) in enumerate(products):
                        last = T.matmul(bank[b][:, 0:2 * n].rearrange("p (h c) -> p h c", h=2),
                                        key[:, first:first + P], query[:, :, first:first + n],
                                        start=(m == 0), stop=(m == 2))
                    last.then_inc(full[b], 1)

                def retrieve():
                    wait_free(eng, "retrieved", i)
                    for seq in range(2):
                        wait_taken(eng, f"scores{seq}_late", i)
                        for part in range(2):
                            for half in range(2):
                                last = T.matmul(
                                    bank[2][half * D:(half + 1) * D, seq * SEQ + part * P:(seq + 1) * SEQ],
                                    value[:, 4 * half + 2 * seq + part, :],
                                    attn[:, seq, half, (0 if part == 0 else SEQ):SEQ + part * P],
                                    start=(part == 0), stop=(part == 1), skip_group_check=True)
                    last.then_inc(full[2], 1)

                def up(*which):
                    for n in which:
                        if ffn:
                            half, part = divmod(n, 2)
                            job = f"up{n}"
                            wait_taken(eng, f"ffn_in{half}", i)
                            wait_free(eng, job, i)
                            cols = slice(part * P, (part + 1) * P)
                            two_parts(bank[BANK_OF[job]][:, :], up_hi[:, cols], up_lo[:, cols],
                                      normed_t[2][:, half * HALF:(half + 1) * HALF])\
                                .then_inc(full[BANK_OF[job]], 1)

                def convolve():
                    if conv:
                        if isinstance(i, int) and i == 0:
                            eng.wait_ge(s_conv_ready, 1)
                        wait_taken(eng, "window8", i)
                        wait_taken(eng, "window9", i)
                        by_halves("conv", lambda k: conv_wt[:, k, :], lambda k: window_t[:, k, :], i,
                                  (P,) * (BLOCKS - 1) + (TAIL,))

                def conv_back():
                    if conv:
                        wait_taken(eng, "conv", i)
                        channel_to_token(conv_ch, "conv_tok", i)

                def gate():
                    if ffn:
                        wait_taken(eng, "up3", i)
                        wait_free(eng, "gate", i)
                        for half in range(2):
                            for k in range(2):
                                row = (2 * half + k) * QUADRANT
                                last = T.matmul(bank[4][row:row + QUADRANT, :], gate_w[:, k, :],
                                                act[:, k, half * HALF:(half + 1) * HALF], start=True, stop=True)
                        last.then_inc(full[4], 1)

                def encode(half):
                    if features:
                        job = f"hidden{half}"
                        wait_taken(eng, f"attn_in{half}", i)
                        wait_free(eng, job, i)
                        two_parts(bank[BANK_OF[job]][:, :], kq_hi[:, :], kq_lo[:, :],
                                  normed_t[1][:, half * HALF:(half + 1) * HALF])\
                            .then_inc(full[BANK_OF[job]], 1)

                def values(half):
                    if features:
                        job = f"value{half}"
                        b = BANK_OF[job]
                        wait_free(eng, job, i)
                        for s in range(4):
                            cols = slice((4 * half + s) * P, (4 * half + s + 1) * P)
                            n = 2 * P if s < 3 else P
                            last = T.matmul(bank[b][:, s * P:s * P + n], normed_t[1][:, cols], v_parts[:, 0:n],
                                            start=True, stop=True)
                        last.then_inc(full[b], 1)

                if filling(i):
                    windows(0, 1, 2, 3, 4, 5, 6)
                    scores(0, "early")
                    scores(0, "late")
                    windows(7, 8)
                    scores(1, "early")
                    windows(9)
                    if early(i):
                        convolve()
                else:
                    if ffn:
                        if isinstance(i, int) and i == LAG_FFN:
                            eng.wait_ge(s_weights_ready, 7)
                            eng.wait_ge(s_ffn_loads, 16 * FFN_LOADS)
                        eng.wait_ge(normed_ready[2], i - LAG_FFN + 1)
                        token_to_channel(normed[2], "ffn_in0", i)
                        token_to_channel(normed[2], "ffn_in1", i)
                    windows(0)
                    scores(0, "early")
                    up(0, 1)
                    windows(1)
                    scores(0, "late")
                    up(2, 3)
                    scores(1, "early")
                    windows(2)
                if features:
                    g = i - LAG_FEATURES
                    if isinstance(g, int) and g == 0:
                        eng.wait_ge(s_weights_ready, 3)
                        eng.wait_ge(s_feature_loads, 16 * FEATURE_LOADS)
                    eng.wait_ge(normed_ready[1], g + 1)
                    token_to_channel(normed[1], "attn_in0", i)
                    token_to_channel(normed[1], "attn_in1", i)
                if early(i):
                    conv_back()
                scores(1, "late")
                if attend:
                    retrieve()
                gate()
                if attend:
                    wait_taken(eng, "retrieved", i)
                    channel_to_token(retrieved, "retrieved_tok", i)
                encode(1)
                later_windows(3)
                encode(0)
                later_windows(4)
                if ffn:
                    wait_taken(eng, "gate", i)
                    channel_to_token(logits_ch, "gate_tok", i)
                later_windows(5)
                values(0)
                later_windows(6, 7)
                values(1)
                experts(0)
                later_windows(8, 9)
                experts(1)
                if ffn:
                    eng.wait_ge(weight_split, i - LAG_FFN + 1)
                    wait_free(eng, "weights_ch", i)
                    T.transpose(bank[3][:, 0:P], weight_parts[:, :, :, :].rearrange("p a t e -> p (a t e)"),
                                ident[:, :]).then_inc(full[3], 1)
                experts(2)
                if features:
                    wait_taken(eng, "hidden0", i)
                    by_halves("phase_k", lambda k: phase_k_w[:, :], lambda k: hidden[:, :], i)
                    by_halves("phase_q", lambda k: phase_q_w[:, :], lambda k: hidden[:, :], i)
                if ffn:
                    wait_taken(eng, "weights_ch", i)
                    wait_free(eng, "down_bias", i)
                    T.matmul(bank[2][:, :], weight_ch[:, :], down_b_hi[:, :], start=True, stop=False)
                    T.matmul(bank[2][:, :], weight_ch[:, :], down_b_lo[:, :], start=False, stop=True)\
                        .then_inc(full[2], 1)
                experts(3, 4)
                if not early(i):
                    convolve()
                experts(5)
                if not early(i):
                    conv_back()
                experts(6, 7)

            emit(body)(pe)

    return nc


def kernel(**inputs):
    import numpy as _np
    import concourse.bacc as _bacc
    from concourse import mybir as _mybir
    from concourse.bass_utils import run_bass_kernel_spmd as _run

    def t(name):
        return _np.ascontiguousarray(_np.transpose(_np.asarray(inputs[name])))

    def plain(name):
        return _np.ascontiguousarray(_np.asarray(inputs[name]))

    conv_w = _np.asarray(inputs["L0_tok_W"])
    arrays = {
        "x": plain("x").reshape(-1),
        "emb": plain("L0_tok_emb"),
        "conv_w": _np.ascontiguousarray(_np.transpose(conv_w, (2, 1, 0))).reshape(WINDOW, D),
        "conv_b": plain("L0_tok_b"),
        "kw1": t("L0_attn_kw1"), "kb1": plain("L0_attn_kb1"), "kw2": t("L0_attn_kw2"), "kb2": plain("L0_attn_kb2"),
        "qw1": t("L0_attn_qw1"), "qb1": plain("L0_attn_qb1"), "qw2": t("L0_attn_qw2"), "qb2": plain("L0_attn_qb2"),
        "vw": t("L0_attn_vw"), "vb": plain("L0_attn_vb"),
        "w1": plain("L0_ffn_W1"), "b1": plain("L0_ffn_b1"), "wg": plain("L0_ffn_Wg"), "bg": plain("L0_ffn_bg"),
        "wd": plain("L0_ffn_Wd"), "bd": plain("L0_ffn_bd"),
    }
    nc = _bacc.Bacc("TRN2", target_bir_lowering=False, num_devices=1)
    args = [nc.dram_tensor(f"in_{n}", a.shape, _mybir.dt.from_np(a.dtype), kind="ExternalInput").ap()
            for n, a in arrays.items()]
    out = nc.dram_tensor("out_h", (TOKENS, D), _mybir.dt.float32, kind="ExternalOutput").ap()
    build(nc, *args, out)
    r = _run(nc, [{f"in_{n}": a for n, a in arrays.items()}], core_ids=[0])
    return r.results[0]["out_h"].reshape(BATCH, SEQ, D)
```
